# Optimizing a Trainium2 kernel written in Bass

```python
import numpy as np
import jax
import jax.numpy as jnp

def _softmax(x, axis=-1):
    return jax.nn.softmax(x, axis=axis)

def _gelu(x):
    return jax.nn.gelu(x, approximate=True)

def _silu(x):
    return jax.nn.silu(x)

def _sigmoid(x):
    return jax.nn.sigmoid(x)

def _layernorm(x, axis=-1, eps=1e-05):
    m = jnp.mean(x, axis=axis, keepdims=True)
    v = jnp.var(x, axis=axis, keepdims=True)
    return (x - m) / jnp.sqrt(v + eps)

def _scatter_add(tgt, idx, src, axis=0):
    return tgt.at[idx].add(src)

def _segment_sum(src, seg, n):
    return jax.ops.segment_sum(src, seg, n)
kernel_name = 'mk_gnn_resnorm_d2_gnn_r32_9b8321'

def setup_inputs(seed: int=0):
    np.random.seed(seed)
    _w = jnp.asarray

    def _rec_inputs():
        import jax
        import jax.numpy as jnp
        _gk = jax.random.key(seed)
        x = -0.0003713 + 1 * jax.random.normal(jax.random.fold_in(_gk, 1), (3125, 128), jnp.float32)
        _s = jax.random.randint(jax.random.fold_in(_gk, 2), (50000,), 0, 3125, jnp.int32)
        _d = jax.random.randint(jax.random.fold_in(_gk, 3), (50000,), 0, 3125, jnp.int32)
        _loop = jnp.arange(3125, dtype=jnp.int32)
        src = jnp.concatenate([_s, _d, _loop])
        dst = jnp.concatenate([_d, _s, _loop])
        _o = jnp.argsort(dst, stable=True)
        src = src[_o]
        dst = dst[_o]
        edge_type_8 = jax.random.randint(jax.random.fold_in(_gk, 13), (103125,), 0, 8, jnp.int32)
        edge_weight = jax.random.uniform(jax.random.fold_in(_gk, 14), (103125,), jnp.float32, 0.0, 1)
        return (x, src, dst, edge_type_8, edge_weight)
    x, src, dst, edge_type_8, edge_weight = _rec_inputs()

    def _L0_gnn_setup():
        import jax, jax.numpy as jnp
        import numpy as np
        N = 3125
        E = 50000
        D = 128
        L = 3
        OUT = 128
        key = jax.random.key(seed)
        ks = jax.random.split(key, 6)
        x = jax.random.normal(ks[0], (N, D), dtype=jnp.float32)
        edge_index = jax.random.randint(ks[1], (2, E), 0, N, dtype=jnp.int64)
        s = 1.0 / np.sqrt(D)
        conv_w = jax.random.normal(ks[2], (L, D, D), dtype=jnp.float32) * s
        conv_b = jax.random.normal(ks[3], (L, D), dtype=jnp.float32) * 0.01
        lin_w = jax.random.normal(ks[4], (OUT, D * (L + 1)), dtype=jnp.float32) * (1.0 / np.sqrt(D * (L + 1)))
        lin_b = jax.random.normal(ks[5], (OUT,), dtype=jnp.float32) * 0.01
        return {'x': x, 'edge_index': edge_index, 'conv_w': conv_w, 'conv_b': conv_b, 'lin_w': lin_w, 'lin_b': lin_b}
    _L0_gnn_all = _L0_gnn_setup()
    _L0_gnn_in = {k: v for k, v in _L0_gnn_all.items() if k in ('conv_w', 'conv_b', 'lin_w', 'lin_b')}
    del _L0_gnn_all

    def _L1_gnn_setup():
        import jax, jax.numpy as jnp
        import numpy as np
        N_NODES = 50000
        N_EDGES = 25000
        N_RELS = 8
        N_BASES = 4
        IN_FEAT = 128
        OUT_FEAT = 128
        key = jax.random.key(seed)
        k = jax.random.split(key, 7)
        x = jax.random.normal(k[0], (N_NODES, IN_FEAT), dtype=jnp.float32)
        edge_norm = jax.random.uniform(k[1], (N_EDGES,), dtype=jnp.float32)
        bases = jax.random.normal(k[2], (N_BASES, IN_FEAT, OUT_FEAT), dtype=jnp.float32) * 0.05
        w_comp = jax.random.normal(k[3], (N_RELS, N_BASES), dtype=jnp.float32)
        edge_src = jax.random.randint(k[4], (N_EDGES,), 0, N_NODES, dtype=jnp.int32)
        edge_dst = jax.random.randint(k[5], (N_EDGES,), 0, N_NODES, dtype=jnp.int32)
        edge_type = jax.random.randint(k[6], (N_EDGES,), 0, N_RELS, dtype=jnp.int32)
        return {'x': x, 'edge_norm': edge_norm, 'bases': bases, 'w_comp': w_comp, 'edge_src': edge_src, 'edge_dst': edge_dst, 'edge_type': edge_type}
    _L1_gnn_all = _L1_gnn_setup()
    _L1_gnn_in = {k: v for k, v in _L1_gnn_all.items() if k in ('bases', 'w_comp')}
    del _L1_gnn_all
    return {'x': x, 'src': src, 'dst': dst, 'edge_type_8': edge_type_8, 'edge_weight': edge_weight, 'L0_gnn_conv_w': _L0_gnn_in['conv_w'], 'L0_gnn_conv_b': _L0_gnn_in['conv_b'], 'L0_gnn_lin_w': _L0_gnn_in['lin_w'], 'L0_gnn_lin_b': _L0_gnn_in['lin_b'], 'L1_gnn_bases': _L1_gnn_in['bases'], 'L1_gnn_w_comp': _L1_gnn_in['w_comp']}

def reference(x, src, dst, edge_type_8, edge_weight, L0_gnn_conv_w, L0_gnn_conv_b, L0_gnn_lin_w, L0_gnn_lin_b, L1_gnn_bases, L1_gnn_w_comp):
    import jax
    import jax.numpy as jnp

    def _L0_gnn_ref(x, edge_index, conv_w, conv_b, lin_w, lin_b):
        import jax, jax.numpy as jnp
        import numpy as np
        N = 3125
        E = 50000
        D = 128
        L = 3
        OUT = 128
        n = x.shape[0]
        loop = jnp.arange(n, dtype=edge_index.dtype)
        src = jnp.concatenate([edge_index[0], loop])
        dst = jnp.concatenate([edge_index[1], loop])
        deg = jax.ops.segment_sum(jnp.ones_like(src, dtype=x.dtype), dst, num_segments=n)
        dinv = jnp.where(deg > 0, jax.lax.rsqrt(deg), 0.0)
        norm = (dinv[src] * dinv[dst])[:, None]

        def gcn_conv(h, W, b):
            hw = h @ W.T
            msg = hw[src] * norm
            agg = jax.ops.segment_sum(msg, dst, num_segments=n)
            return agg + b
        h_list = [x]
        for l in range(conv_w.shape[0]):
            h = jax.nn.elu(gcn_conv(h_list[l], conv_w[l], conv_b[l]))
            h = h + h_list[l]
            h_list.append(h)
        node_repr = jnp.concatenate(h_list, axis=1)
        return node_repr @ lin_w.T + lin_b

    def _L1_gnn_ref(x, edge_norm, bases, w_comp, edge_src, edge_dst, edge_type):
        import jax, jax.numpy as jnp
        import numpy as np
        N_NODES = 50000
        N_EDGES = 25000
        N_RELS = 8
        N_BASES = 4
        IN_FEAT = 128
        OUT_FEAT = 128
        N = x.shape[0]
        R = w_comp.shape[0]
        W = jnp.einsum('rb,bio->rio', w_comp, bases)
        msg = x[edge_src] * edge_norm[:, None]
        seg = edge_type * N + edge_dst
        agg = jax.ops.segment_sum(msg, seg, num_segments=R * N)
        agg = agg.reshape(R, N, -1)
        out = jnp.einsum('rni,rio->no', agg, W)
        return out
    edge_index = jnp.stack([src, dst])
    x = _layernorm(x + _L0_gnn_ref(x, edge_index, L0_gnn_conv_w, L0_gnn_conv_b, L0_gnn_lin_w, L0_gnn_lin_b), axis=-1)
    x = _layernorm(x + _L1_gnn_ref(x, edge_weight, L1_gnn_bases, L1_gnn_w_comp, src, dst, edge_type_8), axis=-1)
    return x

_drawn_inputs = setup_inputs


def setup_inputs(seed=0):
    import zlib

    import numpy as np

    out = dict(_drawn_inputs(seed))
    spreads = {}
    factors = {'L0_gnn_conv_b': 3.571, 'L0_gnn_lin_b': 3.657}
    for name, (base, spread) in spreads.items():
        noise = np.random.default_rng([zlib.crc32(name.encode()), seed]).standard_normal(out[name].shape)
        drawn = base * np.exp(spread * noise) if base else spread * noise
        out[name] = jnp.asarray(drawn.astype(out[name].dtype))
    for name, factor in factors.items():
        out[name] = (out[name] * factor).astype(out[name].dtype)
    return out
```

```python
import concourse.bass as bass
from concourse import mybir
from contextlib import ExitStack


def build_program(nc, x, src, dst, etype, eweight, conv_w, conv_b, lin_w, lin_b, bases, w_comp, out):
    fp32, bf16 = mybir.dt.float32, mybir.dt.bfloat16
    i32, u32 = mybir.dt.int32, mybir.dt.uint32
    ALU = mybir.AluOpType
    ACT = mybir.ActivationFunctionType
    AX = mybir.AxisListType
    ds = bass.ds

    P = 128
    N, D = x.shape
    E = src.shape[0]
    LAYERS = conv_w.shape[0]
    RELS, NB = w_comp.shape
    BLK = 125
    NBLK = N // BLK
    TILES = E // BLK
    TPB = TILES // NBLK
    assert N == NBLK * BLK and E == TILES * BLK and TILES == TPB * NBLK
    BW = 5
    QW = BW * NBLK
    WIN = 256
    WUSE = WIN - 1
    UB = 5
    NBUK = UB * P
    SSTEP = 165
    NSMP = E // SSTEP // BLK
    GRP = 4
    GN = GRP * BW
    NGRP = -(-(N // BW) // GRP)
    CH = 480
    GPC = CH // GN
    NCH = -(-N // CH)
    LASTG = NGRP - GPC * (NCH - 1)
    CW = [CH] * (NCH - 1) + [N - CH * (NCH - 1)]
    SW = [CH] * (NCH - 1) + [LASTG * GN]
    COFF = [CH * NBLK * c for c in range(NCH)]
    ADJ = COFF[-1] + NBLK * SW[-1]
    UBT = 4
    NUB = -(-NBLK // UBT)
    WN = 48
    WBACK = 21
    LO = [BLK * j // TPB - WBACK for j in range(TPB)]
    MAGIC = 12582912.0
    EPS = 1e-5
    BIG = 6 * P
    TAILR = TILES - BIG

    ctx = ExitStack()
    with ctx:
        def sb(name, shape, dt):
            return ctx.enter_context(nc.sbuf_tensor(name, shape, dt))

        def sem(name):
            return ctx.enter_context(nc.semaphore(name))

        adj = sb("adj", [P, ADJ], bf16)
        hT = sb("hT", [P, N], fp32)
        dinv_all = sb("dinv_all", [P, N], fp32)
        u = sb("u", [P, NBLK, 3, D], bf16)
        work = sb("work", [P, 3, UBT * D], fp32)
        wT = sb("wT", [P, LAYERS, D], fp32)
        linT = sb("linT", [P, LAYERS + 1, D], fp32)
        convb = sb("convb", [P, LAYERS], fp32)
        ident = sb("ident", [P, P], fp32)
        ones = sb("ones", [P, P], bf16)
        onesf = sb("onesf", [P, 1], fp32)
        dinv_col = sb("dinv_col", [P, NBLK], fp32)
        thr_g = sb("thr_g", [P, UB], fp32)
        idx_s = sb("idx_s", [P, UB], u32)
        idx_w = sb("idx_w", [P, UB], u32)
        pos = sb("pos", [P, 3, UB], fp32)
        deg = sb("deg", [P, UB, BW], fp32)
        totals = sb("totals", [P, 2], fp32)
        flagf = sb("flagf", [P, 3], fp32)
        flag = sb("flag", [P, 1], i32)
        epst = sb("epst", [P, 1], fp32)
        compB = sb("compB", [P, RELS * NB], fp32)

        def carve(byte, cols, dt, size):
            return adj[:, byte // 2:(byte + cols * size) // 2].bitcast(dt)

        dstP = carve(0, TILES, i32, 4)
        thr = carve(3300 + 28, NBUK, fp32, 4)
        cmp = adj[:, 3200:3200 + UB * NBUK].rearrange("p (k g) -> p k g", k=UB)
        samp = carve(12800, 32, fp32, 4)
        swin = carve(13056, UB * SSTEP, i32, 4).rearrange("p (b e) -> p b e", b=UB)
        swinf = carve(16384, UB * SSTEP, fp32, 4).rearrange("p (b e) -> p b e", b=UB)
        EW = UB * WIN
        dwin = carve(20480, EW, i32, 4).rearrange("p (b e) -> p b e", b=UB)
        ewin = carve(25600, EW, i32, 4).rearrange("p (b e) -> p b e", b=UB)
        dwf = carve(30720, EW, fp32, 4).rearrange("p (b e) -> p b e", b=UB)
        swf = carve(35840, EW, fp32, 4).rearrange("p (b e) -> p b e", b=UB)
        hif = carve(40960, EW, fp32, 4).rearrange("p (b e) -> p b e", b=UB)
        junk = carve(46080, 1024, fp32, 4)
        RAW = 7 * BLK
        raws = [carve(72000 + 3520 * a, RAW, dt, 4).rearrange("p (b e) -> p b e", b=7)
                for a, dt in enumerate((i32, i32, i32, fp32))]
        rawf = [carve(86400 + 3520 * a, RAW, fp32, 4).rearrange("p (b e) -> p b e", b=7) for a in range(3)] + [raws[3]]
        edgeT = [carve(97280 + 3328 * a, TILES, dt, 4) for a, dt in enumerate((fp32, u32, fp32, fp32))]
        baseT = carve(110720, TILES, fp32, 4)
        dlT = carve(114048, TILES, fp32, 4)
        inT = carve(117376, TILES, fp32, 4)
        wst = carve(121600, LAYERS * D, fp32, 4).rearrange("p (l d) -> p l d", l=LAYERS)
        lst = carve(123392, (LAYERS + 1) * D, fp32, 4)
        iota_f = carve(126976, P, fp32, 4)
        xst = carve(COFF[-1] * 2, NBLK * D, fp32, 4).rearrange("p (s d) -> p s d", s=NBLK)
        uflat = u[:, :, :, :].rearrange("p s k d -> p (s k d)")
        sT = [uflat[:, 1280 * a:1280 * (a + 1)] for a in range(2)]
        OHC = P * GRP * 2
        hot = [[uflat[:, 2560 + OHC * (2 * s + a):2560 + OHC * (2 * s + a + 1)].rearrange("p (v t) -> p v t", t=8)
                for a in range(2)] for s in range(2)]
        iota_v = uflat[:, 2560 + 4 * OHC:2560 + 5 * OHC].rearrange("p (v t) -> p v t", t=8)
        RB = CH * NBLK * 2
        h_old = [carve(RB * l, N, fp32, 4) for l in range(LAYERS)]
        basesS = carve(12544, NB * D, fp32, 4).rearrange("p (b d) -> p b d", b=NB)
        srcI = carve(14592, TILES, u32, 4)
        dl = carve(17920, TILES, fp32, 4)
        wE = carve(RB + 12544, TILES, fp32, 4)
        tyE = carve(RB + 15872, TILES, fp32, 4)
        linbB = carve(RB + 19200, D, fp32, 4)
        coef = carve(3 * RB, TILES * NB, fp32, 4).rearrange("p (t b) -> p t b", b=NB)
        relw = carve(3 * RB + 13312, TILES, fp32, 4)
        xb = carve(4 * RB, NBLK * D, fp32, 4).rearrange("p (s d) -> p s d", s=NBLK)
        acc = carve(4 * RB + 12800, NB * BLK, fp32, 4)
        carry = carve(4 * RB + 14848, NB * BLK, fp32, 4)
        aggf = carve(4 * RB + 16896, NB * BLK, fp32, 4).rearrange("p (b n) -> p b n", b=NB)
        bnst = carve(4 * RB + 18944, UBT * 8, fp32, 4).rearrange("p (t s) -> p t s", t=UBT)
        mv = carve(4 * RB + 19072, NBLK * 2, fp32, 4).rearrange("p (t s) -> p t s", s=2)
        rstd = carve(4 * RB + 19328, NBLK, fp32, 4)
        iota_w = carve(4 * RB + 19456, WN, fp32, 4)
        iota_wf = carve(4 * RB + 19712, P, fp32, 4)
        ystage = carve(4 * RB + 20480, 2 * D, fp32, 4).rearrange("p (s d) -> p s d", s=2)
        fst = carve(4 * RB + 21504, 16, fp32, 4)
        idxg = carve(4 * RB + 21632, TPB, u32, 4)
        gat = carve(5 * RB, TPB * D, fp32, 4).rearrange("p (j d) -> p j d", j=TPB)
        MS = 3
        mov = carve(5 * RB + 17408, MS * NB * WN, fp32, 4).rearrange("p (s b w) -> p s b w", s=MS, b=NB)
        zeros = adj[:, (5 * RB + 20480) // 2:(5 * RB + 20480) // 2 + 512]

        H4 = 12544
        g_h = [carve(H4 * l, N, fp32, 4) for l in range(LAYERS)]
        g_hs = carve(H4 * 3, N, fp32, 4)
        g_iota = carve(H4 * 4, N, fp32, 4)
        g_hot = carve(H4 * 5, N, fp32, 4)
        G0 = H4 * 6
        g_dst, g_src, g_w, g_ty = [carve(G0 + 3328 * a, TILES, dt, 4) for a, dt in enumerate((fp32, u32, fp32, fp32))]
        g_relw = carve(G0 + 4 * 3328, TILES, fp32, 4)
        g_coef = carve(G0 + 5 * 3328, TILES * NB, fp32, 4).rearrange("p (t b) -> p t b", b=NB)
        g_xb = carve(G0 + 33280, NBLK * D, fp32, 4).rearrange("p (s d) -> p s d", s=NBLK)
        g_tab = carve(G0 + 46080, NBLK * D, fp32, 4).rearrange("p (s d) -> p s d", s=NBLK)
        g_rows = carve(G0 + 58880, D, fp32, 4)
        g_linb = carve(G0 + 59392, D, fp32, 4)
        g_bases = carve(G0 + 59904, NB * D, fp32, 4).rearrange("p (b d) -> p b d", b=NB)
        g_bn = carve(G0 + 61952, 8, fp32, 4)
        g_mv = carve(G0 + 61984, NBLK * 2, fp32, 4).rearrange("p (t s) -> p t s", s=2)
        g_std = carve(G0 + 62208, 32, fp32, 4)
        g_idx1 = carve(G0 + 62336, 8, u32, 4)
        g_nop = carve(G0 + 62368, 8, fp32, 4)
        g_zero = carve(G0 + 62400, P, fp32, 4)

        table_d = nc.dram_tensor("table_scratch", [N, D], fp32, kind="Internal").ap()
        dinv_d = nc.dram_tensor("dinv_scratch", [NBUK * BW], fp32, kind="Internal").ap()
        edge_d = [nc.dram_tensor(f"edge_scratch{a}", [BLK, TILES], dt, kind="Internal").ap()
                  for a, dt in enumerate((fp32, u32, fp32, fp32, fp32))]
        h_d = [nc.dram_tensor(f"h_scratch{l}", [P, N], fp32, kind="Internal").ap() for l in range(LAYERS)]
        x1_d = nc.dram_tensor("x1_scratch", [N, D], fp32, kind="Internal").ap()

        ps = ctx.enter_context(nc.psum_tensor("ps", [P, 8, 512], fp32))

        s_dst = sem("dst_loaded")
        s_raw = [sem(f"edges_loaded{a}") for a in range(4)]
        s_x = sem("x_loaded")
        s_wl = sem("weights_loaded")
        s_iota = sem("iotas_made")
        s_const = sem("constants_made")
        s_cmp = sem("samples_compared")
        s_cnt = sem("samples_counted")
        s_idxs = sem("sample_windows_known")
        s_swin = sem("sample_windows_loaded")
        s_idxw = sem("bucket_windows_known")
        s_bwin = sem("bucket_windows_loaded")
        s_rawf = sem("edges_as_floats")
        s_job = sem("transposed")
        s_ev = sem("transposes_copied")
        s_win = sem("window_codes_ready")
        s_deg = sem("degrees_ready")
        s_sq = sem("sqrt_ready")
        s_dinv = sem("dinv_ready")
        s_dinvd = sem("dinv_stored")
        s_dinvl = sem("dinv_loaded")
        s_dl = sem("window_places_ready")
        s_edst = sem("edges_stored")
        s_tot = sem("totals_ready")
        s_totp = sem("totals_summed")
        s_hot = sem("onehots_ready")
        s_blk = sem("bucket_blocks_ready")
        s_adj = sem("adjacency_written")
        s_eye = sem("self_loops_added")
        s_w = sem("hw_ready")
        s_uf = sem("u_scaled")
        s_hi = sem("u_part0")
        s_r1 = sem("u_rest1")
        s_mid = sem("u_part1")
        s_u = sem("u_ready")
        s_agg = sem("aggregated")
        s_rd = sem("aggregate_read")
        s_exp = sem("exp_ready")
        s_h = sem("h_ready")
        s_hs = sem("h_stored")
        s_back = [sem(f"reloaded{r}") for r in range(6)]
        s_xb = sem("x_plus_bias")
        s_lin = sem("lin_ready")
        s_var = sem("variance_ready")
        s_std = sem("std_ready")
        s_x1 = sem("x1_ready")
        s_x1d = sem("x1_stored")
        s_idx = sem("indices_ready")
        s_g = [sem(f"gathered{g}") for g in range(3)]
        s_m = sem("moving_ready")
        s_mu = sem("tile_done")
        s_zero = sem("zeros_made")
        s_fold = sem("chunk_folded")
        s_af = sem("chunk_sum_ready")
        s_fin = sem("chunk_transformed")
        s_fv = sem("chunk_variance")
        s_fs = sem("chunk_std")
        s_y = sem("chunk_normalised")
        s_out = sem("chunk_stored")
        s_flag = sem("flag_ready")
        s_vch = sem("dve_chain")
        s_ach = sem("act_chain")
        s_pch = sem("pool_chain")

        e_ld = sem("g_loaded")
        e_io = sem("g_constants_made")
        e_idx = sem("g_indices_ready")
        e_hot = sem("g_onehots_ready")
        e_ga = [sem(f"g_rows_gathered{p}") for p in range(LAYERS + NB)]
        e_mm = sem("g_tile_done")
        e_sq = sem("g_sqrt_ready")
        e_dinv = sem("g_dinv_ready")
        e_hs = sem("g_scaled_h_ready")
        e_tab = sem("g_table_blocks_made")
        e_tc = sem("g_table_blocks_copied")
        e_td = sem("g_table_stored")
        e_min = sem("g_min_ready")
        e_exp = sem("g_exp_ready")
        e_h = sem("g_h_ready")
        e_lin = sem("g_product_ready")
        e_lc = sem("g_product_taken")
        e_var = sem("g_variance_ready")
        e_std = sem("g_std_ready")
        e_x1 = sem("g_x1_ready")
        e_x1d = sem("g_x1_stored")
        e_agg = sem("g_aggregate_copied")
        e_y = sem("g_result_ready")
        e_out = sem("g_result_stored")
        e_nop = sem("g_wait_taken")

        GG = TPB // 3
        NJ = 2 + 8 + NCH + 6
        HX = NUB * 1

        def cover(j):
            need = min(N, (j + 1) * UBT * BLK)
            return -(-need // CH)

        def blocks_of(j):
            return range(UBT * j, min(NBLK, UBT * (j + 1)))

        block = ctx.enter_context(nc.Block())

        GC = UBT * BLK
        GW = [min(N, GC * (c + 1)) - GC * c for c in range(NUB)]
        PASSES = 1 + LAYERS + NB

        def general_sp(sp):
            sp.wait_ge(s_ev, NJ)
            sp.wait_ge(s_edst, 80)
            sp.wait_ge(s_tot, 2)
            for t, a in ((g_dst, 4), (g_src, 1), (g_w, 3), (g_ty, 2)):
                sp.dma_start(t[0:BLK], edge_d[a]).then_inc(e_ld, 16)
            sp.dma_start(g_bases[:, :, :], bases.rearrange("b i o -> i b o")).then_inc(e_ld, 16)
            sp.dma_start(g_linb[:, :], lin_b.rearrange("(o d) -> o d", o=1).broadcast_to([P, D])).then_inc(e_ld, 16)
            sp.dma_start(g_xb[0:BLK], x.rearrange("(s p) d -> p s d", p=BLK)).then_inc(e_ld, 16)
            for l in range(LAYERS):
                sp.wait_ge(e_tc, NUB * (l + 1))
                sp.dma_start(table_d.rearrange("(s p) d -> p s d", p=BLK), g_tab[0:BLK]).then_inc(e_td, 16)
            sp.wait_ge(e_x1, 1)
            sp.dma_start(x1_d.rearrange("(s p) d -> p s d", p=BLK), g_xb[0:BLK]).then_inc(e_x1d, 16)
            sp.wait_ge(e_y, 1)
            sp.dma_start(out.rearrange("(s p) d -> p s d", p=BLK), g_tab[0:BLK]).then_inc(e_out, 16)
            sp.wait_ge(e_out, 16)

        def general_pool(pool):
            pool.wait_ge(s_ev, NJ)
            pool.wait_ge(s_tot, 2)
            pool.wait_ge(s_edst, 80)
            nc.gpsimd.iota(g_iota[:, :], pattern=[[1, N]], base=0, channel_multiplier=0, allow_small_or_imprecise_dtypes=True).then_inc(e_io, 1)
            nc.gpsimd.memset(g_rows[:, :], 1.0).then_inc(e_io, 1)
            nc.gpsimd.memset(g_zero[:, :], 0.0).then_inc(e_io, 1)
            nc.gpsimd.memset(g_nop[:, :], 0.0).then_inc(e_nop, 1)
            for p in range(1, PASSES):
                table = table_d if p <= LAYERS else x1_d
                if p <= LAYERS:
                    pool.wait_ge(e_td, 16 * p)
                else:
                    pool.wait_ge(e_x1d, 16)
                with pool.Fori(0, TILES) as t:
                    pool.wait_ge(e_idx, t + (TILES * (p - 1) + 1))
                    pool.wait_ge(e_nop, t + (TILES * (p - 1) + 1))
                    nc.gpsimd.tensor_tensor(g_nop[:, 0:1], epst[:, 0:1], epst[:, 0:1], ALU.add).then_inc(e_nop, 1)
                    nc.gpsimd.indirect_dma_start(out=g_rows[0:BLK, :], out_offset=None, in_=table,
                                                 in_offset=bass.IndirectOffsetOnAxis(ap=g_idx1[0:BLK, 0:1], axis=0)).then_inc(e_ga[p - 1], 16)

        def general_act(act):
            act.wait_ge(e_mm, TILES + 1)
            for c in range(NUB):
                ins = nc.scalar.activation(dinv_all[:, GC * c:GC * c + GW[c]], ps[:, c, 0:GW[c]], ACT.Sqrt, bias=onesf[:, 0:1])
                ins.then_inc(e_sq, 1)
            for l in range(LAYERS):
                for c in range(NUB):
                    act.wait_ge(e_min, NUB * l + c + 1)
                    nc.scalar.activation(work[:, 1, 0:GW[c]], work[:, 1, 0:GW[c]], ACT.Exp).then_inc(e_exp, 1)
            for r in range(2):
                act.wait_ge(e_var, r + 1)
                nc.scalar.activation(g_std[0:BLK, 0:NBLK], g_mv[0:BLK, :, 1], ACT.Sqrt, bias=epst[0:BLK, 0:1]).then_inc(e_std, 1)

        def general_dve(dve, link):
            V = nc.vector
            dve.wait_ge(e_ld, 16 * 7)
            dve.wait_ge(e_io, 3)
            for r in range(RELS):
                link(V.scalar_tensor_tensor(g_relw[0:BLK, :], g_ty[0:BLK, :], float(r), g_w[0:BLK, :], ALU.is_equal, ALU.mult))
                for b in range(NB):
                    k = compB[0:BLK, r * NB + b:r * NB + b + 1]
                    if r == 0:
                        link(V.tensor_scalar(g_coef[0:BLK, :, b], g_relw[0:BLK, :], k, None, ALU.mult))
                    else:
                        link(V.scalar_tensor_tensor(g_coef[0:BLK, :, b], g_relw[0:BLK, :], k, g_coef[0:BLK, :, b], ALU.mult, ALU.add))

            def onehots(p):
                with dve.Fori(0, TILES) as t:
                    dve.wait_ge(e_mm, t + ((TILES + 1) * p + 1))
                    if p > 0:
                        V.tensor_copy(g_idx1[0:BLK, 0:1], g_src[0:BLK, ds(t, 1)]).then_inc(e_idx, 1)
                    if p <= LAYERS:
                        V.tensor_scalar(g_hot[0:BLK, :], g_iota[0:BLK, :], g_dst[0:BLK, ds(t, 1)], None, ALU.is_equal).then_inc(e_hot, 1)
                    else:
                        co = g_coef[0:BLK, ds(t, 1), p - 1 - LAYERS]
                        V.tensor_scalar(g_hot[0:BLK, :], g_iota[0:BLK, :], g_dst[0:BLK, ds(t, 1)], co, ALU.is_equal, ALU.mult).then_inc(e_hot, 1)
                dve.wait_ge(e_mm, (TILES + 1) * (p + 1))

            onehots(0)
            dve.wait_ge(e_sq, NUB)
            V.reciprocal(dinv_all[:, :], dinv_all[:, :]).then_inc(e_dinv, 1)
            dve.wait_ge(e_dinv, 1)
            for l in range(LAYERS):
                link(V.tensor_copy(g_h[l][:, :], hT[:, :]))
                V.tensor_tensor(g_hs[:, :], hT[:, :], dinv_all[:, :], ALU.mult).then_inc(e_hs, 1)
                for j in range(NUB):
                    b0, nb = blocks_of(j)[0], len(blocks_of(j))
                    dve.wait_ge(e_tab, NUB * l + j + 1)
                    if l > 0 and j == 0:
                        dve.wait_ge(e_td, 16 * l)
                    V.tensor_copy(g_tab[0:BLK, b0:b0 + nb, :], ps[0:BLK, 7, 0:nb * D].rearrange("p (s d) -> p s d", d=D)).then_inc(e_tc, 1)
                onehots(1 + l)
                for c in range(NUB):
                    w, at = GW[c], GC * c
                    z, m, h = work[:, 0, 0:w], work[:, 1, 0:w], hT[:, at:at + w]
                    bias = convb[:, l:l + 1]
                    link(V.tensor_tensor(z, ps[:, c, 0:w], dinv_all[:, at:at + w], ALU.mult))
                    V.tensor_scalar(m, z, bias, 0.0, ALU.add, ALU.min).then_inc(e_min, 1)
                    link(V.tensor_scalar(z, z, bias, 0.0, ALU.add, ALU.max))
                    link(V.tensor_tensor(h, h, z, ALU.add))
                    dve.wait_ge(e_exp, NUB * l + c + 1)
                    V.scalar_tensor_tensor(h, m, -1.0, h, ALU.add, ALU.add).then_inc(e_h, 1)
                    dve.wait_ge(e_h, NUB * l + c + 1)
            link(V.tensor_tensor(g_xb[0:BLK], g_xb[0:BLK], g_linb[0:BLK, None, :].broadcast_to([BLK, NBLK, D]), ALU.add))

            def take(n, j, into):
                b0, nb = blocks_of(j)[0], len(blocks_of(j))
                dve.wait_ge(e_lin, NUB * n + j + 1)
                o = into[0:BLK, b0:b0 + nb, :]
                V.tensor_tensor(o, ps[0:BLK, 7, 0:nb * D].rearrange("p (s d) -> p s d", d=D), o, ALU.add).then_inc(e_lc, 1)

            def norm(r, v):
                for s in range(NBLK):
                    link(V.bn_stats(g_bn[0:BLK, 0:6], v[0:BLK, s, :]))
                    ins = V.bn_aggr(g_mv[0:BLK, s, :], g_bn[0:BLK, 0:6])
                    ins.then_inc(e_var, 1) if s == NBLK - 1 else link(ins)
                dve.wait_ge(e_std, r + 1)
                link(V.reciprocal(g_std[0:BLK, 0:NBLK], g_std[0:BLK, 0:NBLK]))
                for s in range(NBLK):
                    ins = V.tensor_scalar(v[0:BLK, s, :], v[0:BLK, s, :], g_mv[0:BLK, s, 0:1], g_std[0:BLK, s:s + 1], ALU.subtract, ALU.mult)
                    ins.then_inc((e_x1, e_y)[r], 1) if s == NBLK - 1 else link(ins)

            for j in range(NUB):
                take(0, j, g_xb)
            dve.wait_ge(e_lc, NUB)
            norm(0, g_xb)
            dve.wait_ge(e_x1, 1)
            dve.wait_ge(e_td, 16 * LAYERS)
            link(V.tensor_copy(g_tab[0:BLK], g_xb[0:BLK]))
            for b in range(NB):
                onehots(1 + LAYERS + b)
                for c in range(NUB):
                    ins = V.tensor_copy(g_hs[:, GC * c:GC * c + GW[c]], ps[:, c, 0:GW[c]])
                    ins.then_inc(e_agg, 1)
                for j in range(NUB):
                    take(1 + b, j, g_tab)
            dve.wait_ge(e_lc, NUB * (1 + NB))
            norm(1, g_tab)

        def general_pe(pe):
            T = nc.tensor
            pe.wait_ge(e_io, 3)
            pe.wait_ge(e_ld, 16 * 7)

            def tiles(p):
                with pe.Fori(0, TILES) as t:
                    if p > 0:
                        pe.wait_ge(e_ga[p - 1], t * 16 + 16)
                    pe.wait_ge(e_hot, t + (TILES * p + 1))
                    for c in range(NUB):
                        last = T.matmul(ps[:, c, 0:GW[c]], g_rows[0:BLK, :], g_hot[0:BLK, GC * c:GC * c + GW[c]],
                                        start=False, stop=False, skip_group_check=True)
                    last.then_inc(e_mm, 1)

            def clear():
                for c in range(NUB):
                    last = T.matmul(ps[:, c, 0:GW[c]], g_zero[:, :], g_iota[:, 0:GW[c]],
                                    start=True, stop=False, skip_group_check=True)
                last.then_inc(e_mm, 1)
            clear()
            tiles(0)
            for l in range(LAYERS):
                pe.wait_ge(e_hs, l + 1)
                for j in range(NUB):
                    if l + j > 0:
                        pe.wait_ge(e_tc, NUB * l + j)
                    for q, s in enumerate(blocks_of(j)):
                        last = T.matmul(ps[0:BLK, 7, D * q:D * (q + 1)], g_hs[:, BLK * s:BLK * (s + 1)], wT[:, l, :], start=True, stop=True)
                    last.then_inc(e_tab, 1)
                for c in range(NUB):
                    last = T.matmul(ps[:, c, 0:GW[c]], wT[:, l, :], g_hs[:, GC * c:GC * c + GW[c]],
                                    start=True, stop=False, skip_group_check=True)
                last.then_inc(e_mm, 1)
                tiles(1 + l)
                pe.wait_ge(e_h, NUB * (l + 1))
            for j in range(NUB):
                if j == 0:
                    pe.wait_ge(e_tc, NUB * LAYERS)
                else:
                    pe.wait_ge(e_lc, j)
                for q, s in enumerate(blocks_of(j)):
                    for k in range(LAYERS + 1):
                        hk = g_h[k] if k < LAYERS else hT
                        last = T.matmul(ps[0:BLK, 7, D * q:D * (q + 1)], hk[:, BLK * s:BLK * (s + 1)], linT[:, k, :],
                                        start=(k == 0), stop=(k == LAYERS))
                last.then_inc(e_lin, 1)
            for b in range(NB):
                if b > 0:
                    pe.wait_ge(e_agg, NUB * b)
                clear()
                tiles(1 + LAYERS + b)
                pe.wait_ge(e_agg, NUB * (b + 1))
                for j in range(NUB):
                    pe.wait_ge(e_lc, NUB * (1 + b) + j)
                    for q, s in enumerate(blocks_of(j)):
                        last = T.matmul(ps[0:BLK, 7, D * q:D * (q + 1)], g_hs[:, BLK * s:BLK * (s + 1)], g_bases[:, b, :], start=True, stop=True)
                    last.then_inc(e_lin, 1)

        @block.sync
        def _(sp):
            sp.dma_start(dstP[0:BLK, :], dst.rearrange("(p t) -> p t", t=TILES)).then_inc(s_dst, 16)
            for a, arr in enumerate((dst, src, etype, eweight)):
                sp.dma_start(raws[a][:, 0:6, :], arr[0:BIG * BLK].rearrange("(b p e) -> p b e", p=P, e=BLK)).then_inc(s_raw[a], 16)
                sp.dma_start(raws[a][0:TAILR, 6, :], arr[BIG * BLK:E].rearrange("(p e) -> p e", e=BLK)).then_inc(s_raw[a], 16)
            sp.dma_start(wst, conv_w.rearrange("l o i -> o l i")).then_inc(s_wl, 16)
            sp.dma_start(lst, lin_w).then_inc(s_wl, 16)
            with nc.allow_non_contiguous_dma(reason="three short columns"):
                sp.dma_start(convb[:, :], conv_b.rearrange("l d -> d l")).then_inc(s_wl, 16)
            sp.dma_start(compB[:, :], w_comp.rearrange("(o r) b -> o (r b)", o=1).broadcast_to([P, RELS * NB])).then_inc(s_wl, 16)
            sp.dma_start(xst[0:BLK], x.rearrange("(s p) d -> p s d", p=BLK)).then_inc(s_x, 16)
            sp.wait_ge(s_dinv, 1)
            sp.dma_start(dinv_d.rearrange("(b p k) -> p b k", p=P, k=BW), deg[:, :, :]).then_inc(s_dinvd, 16)
            sp.wait_ge(s_dl, 1)
            for a, t in enumerate((dlT, edgeT[1], edgeT[2], edgeT[3], edgeT[0])):
                sp.dma_start(edge_d[a], t[0:BLK, :]).then_inc(s_edst, 16)
            sp.wait_ge(s_dinvd, 16)
            with nc.allow_non_contiguous_dma(reason="a column per row block"):
                sp.dma_start(dinv_col[0:BLK, :], dinv_d[0:N].rearrange("(s p) -> p s", p=BLK)).then_inc(s_dinvl, 16)
            sp.dma_start(dinv_all[:, :], dinv_d[0:N].rearrange("(o n) -> o n", o=1).broadcast_to([P, N])).then_inc(s_dinvl, 16)
            sp.wait_ge(s_flag, 1)
            covered = sp.value_load(flag[0:1, 0:1], min_val=0, max_val=1)
            with sp.If(covered == 1):
                sp.wait_ge(s_ev, 10 + NCH)
                sp.dma_start(h_d[0], hT[:, :]).then_inc(s_hs, 16)
                for l in range(LAYERS - 1):
                    sp.wait_ge(s_h, NCH * (l + 1))
                    sp.dma_start(h_d[l + 1], hT[:, :]).then_inc(s_hs, 16)
                A0 = NCH * (LAYERS - 1)
                sp.wait_ge(s_edst, 80)
                sp.wait_ge(s_hs, 16 * LAYERS)
                sp.wait_ge(s_agg, A0 + 1)
                sp.dma_start(h_old[0], h_d[0]).then_inc(s_back[0], 16)
                sp.dma_start(srcI[0:BLK], edge_d[1]).then_inc(s_back[0], 16)
                sp.dma_start(dl[0:BLK], edge_d[0]).then_inc(s_back[0], 16)
                sp.dma_start(basesS[:, :, :], bases.rearrange("b i o -> i b o")).then_inc(s_back[0], 16)
                sp.wait_ge(s_agg, A0 + 2)
                sp.dma_start(h_old[1], h_d[1]).then_inc(s_back[1], 16)
                sp.dma_start(wE[0:BLK], edge_d[3]).then_inc(s_back[1], 16)
                sp.dma_start(tyE[0:BLK], edge_d[2]).then_inc(s_back[1], 16)
                sp.dma_start(linbB[:, :], lin_b.rearrange("(o d) -> o d", o=1).broadcast_to([P, D])).then_inc(s_back[1], 16)
                sp.wait_ge(s_agg, A0 + 3)
                sp.dma_start(h_old[2], h_d[2]).then_inc(s_back[2], 16)
                sp.wait_ge(s_agg, A0 + 5)
                sp.dma_start(xb[0:BLK], x.rearrange("(s p) d -> p s d", p=BLK)).then_inc(s_back[4], 16)
                for j in range(NUB):
                    b0, b1 = blocks_of(j)[0], blocks_of(j)[-1] + 1
                    sp.wait_ge(s_x1, j + 1)
                    sp.dma_start(x1_d[b0 * BLK:b1 * BLK, :].rearrange("(s p) d -> p s d", p=BLK), xb[0:BLK, b0:b1, :]).then_inc(s_x1d, 16)
                out_v = out.rearrange("(s p) d -> s p d", p=BLK)

                def store(c):
                    sp.wait_ge(s_y, c + 1)
                    sp.dma_start(out_v[c, :, :], ystage[0:BLK, 0, :]).then_inc(s_out, 16)

                with sp.Fori(0, NBLK) as c:
                    sp.wait_ge(s_y, c + 1)
                    sp.dma_start(out_v[ds(c, 1), :, :].rearrange("s p d -> (s p) d"), ystage[0:BLK, 0, :]).then_inc(s_out, 16)
                sp.wait_ge(s_out, 16 * NBLK)
            with sp.Else():
                general_sp(sp)

        @block.gpsimd
        def _(pool):
            nc.gpsimd.iota(thr[:, :], pattern=[[BW, NBUK]], base=0, channel_multiplier=0, allow_small_or_imprecise_dtypes=True).then_inc(s_iota, 1)
            nc.gpsimd.iota(thr_g[:, :], pattern=[[BW * P, UB]], base=0, channel_multiplier=BW, allow_small_or_imprecise_dtypes=True).then_inc(s_iota, 1)
            nc.gpsimd.iota(iota_f[:, :], pattern=[[1, P]], base=0, channel_multiplier=-1, allow_small_or_imprecise_dtypes=True).then_inc(s_iota, 1)
            nc.gpsimd.iota(iota_v[:, :, :], pattern=[[1, P], [0, 8]], base=0, channel_multiplier=0, allow_small_or_imprecise_dtypes=True).then_inc(s_iota, 1)
            nc.gpsimd.iota(baseT[:, :], pattern=[[BLK, TILES]], base=0, channel_multiplier=0, allow_small_or_imprecise_dtypes=True).then_inc(s_iota, 1)
            nc.gpsimd.memset(ones[:, :], 1.0).then_inc(s_const, 1)
            nc.gpsimd.memset(onesf[:, :], 1.0).then_inc(s_const, 1)
            nc.gpsimd.memset(epst[:, :], EPS).then_inc(s_const, 1)
            nc.gpsimd.memset(dwin[:, :, WUSE:WIN], 0).then_inc(s_const, 1)
            nc.gpsimd.memset(ewin[:, :, WUSE:WIN], 0).then_inc(s_const, 1)
            edges_of = [a.rearrange("(n o) -> n o", o=1) for a in (dst, src)]
            pool.wait_ge(s_idxs, 1)
            for b in range(UB):
                nc.gpsimd.indirect_dma_start(out=swin[:, b, :], out_offset=None, in_=edges_of[0],
                                             in_offset=bass.IndirectOffsetOnAxis(ap=idx_s[:, b:b + 1], axis=0)).then_inc(s_swin, 16)
            pool.wait_ge(s_idxw, 1)
            for b in range(UB):
                for a, win in enumerate((dwin, ewin)):
                    nc.gpsimd.indirect_dma_start(out=win[:, b, 0:WUSE], out_offset=None, in_=edges_of[a],
                                                 in_offset=bass.IndirectOffsetOnAxis(ap=idx_w[:, b:b + 1], axis=0)).then_inc(s_bwin, 16)
            pool.wait_ge(s_flag, 1)
            covered = pool.value_load(flag[0:1, 0:1], min_val=0, max_val=1)
            with pool.If(covered == 1):
                pool.wait_ge(s_agg, NCH * (LAYERS - 1) + 5)
                nc.gpsimd.iota(iota_w[:, :], pattern=[[1, WN]], base=0, channel_multiplier=0, allow_small_or_imprecise_dtypes=True).then_inc(s_zero, 1)
                nc.gpsimd.memset(carry[:, :], 0.0).then_inc(s_zero, 1)
                pool.wait_ge(s_agg, NCH * (LAYERS - 1) + 6)
                nc.gpsimd.memset(zeros[:, :], 0.0).then_inc(s_zero, 1)
                pool.wait_ge(s_x1d, 16 * NUB)

                def gathers(c, first):
                    for g in range(3):
                        pool.wait_ge(s_idx, 3 * c + g + 1)
                        if not first:
                            pool.wait_ge(s_mu, TPB * c - TPB + GG * (g + 1))
                        if not first or g:
                            pool.wait_ge(s_pch, c * 3 + g)
                        nc.gpsimd.tensor_tensor(fst[:, 12:13], epst[:, 0:1], epst[:, 0:1], ALU.add).then_inc(s_pch, 1)
                        pool.wait_ge(s_x1d, 16 * NUB)
                        for j in range(GG * g, GG * (g + 1)):
                            nc.gpsimd.indirect_dma_start(out=gat[0:BLK, j, :], out_offset=None, in_=x1_d,
                                                         in_offset=bass.IndirectOffsetOnAxis(ap=idxg[0:BLK, j:j + 1], axis=0)).then_inc(s_g[g], 16)
                gathers(0, True)
                with pool.Fori(1, NBLK) as c:
                    gathers(c, False)
            with pool.Else():
                general_pool(pool)

        @block.scalar
        def _(act):
            for a in range(3):
                act.wait_ge(s_raw[a], 32)
                nc.scalar.copy(rawf[a][:, 0:6, :], raws[a][:, 0:6, :]).then_inc(s_rawf, 1)
                nc.scalar.copy(rawf[a][0:TAILR, 6, :], raws[a][0:TAILR, 6, :]).then_inc(s_rawf, 1)
            n = 0

            def take(dest, rows, cols):
                nonlocal n
                act.wait_ge(s_job, n + 1)
                nc.scalar.copy(dest, ps[0:rows, n % 7, 0:cols]).then_inc(s_ev, 1)
                n += 1
            take(wT[:, :, :].rearrange("p l d -> p (l d)"), P, LAYERS * D)
            take(linT[:, :, :].rearrange("p l d -> p (l d)"), P, (LAYERS + 1) * D)
            for a in range(4):
                take(edgeT[a][0:BLK, 0:512], BLK, 512)
                take(edgeT[a][0:BLK, 512:TILES], BLK, TILES - 512)
            for c in range(NCH):
                w = min(N, 500 * (c + 1)) - 500 * c
                take(hT[:, 500 * c:500 * c + w], P, w)
            act.wait_ge(s_deg, 1)
            nc.scalar.activation(deg[:, :, :], deg[:, :, :], ACT.Sqrt, bias=onesf[:, 0:1]).then_inc(s_sq, 1)
            for a in range(2):
                for q in range(3):
                    nb = min(2, UB - 2 * q)
                    o = sT[a].rearrange("p (b g h) -> p b h g", b=UB, h=2)[:, 2 * q:2 * q + nb, :, :]
                    act.wait_ge(s_job, n + 1)
                    for bb in range(nb):
                        ins = nc.scalar.copy(o[:, bb, :, :], ps[:, n % 7, 256 * bb:256 * bb + 256].rearrange("p (h g) -> p h g", h=2))
                        if bb == nb - 1:
                            ins.then_inc(s_ev, 1)
                        else:
                            ins.then_inc(s_ach, 1)
                    n += 1
            act.wait_ge(s_edst, 80)
            act.wait_ge(s_tot, 2)

            act.wait_ge(s_flag, 1)
            covered = act.value_load(flag[0:1, 0:1], min_val=0, max_val=1)
            with act.If(covered == 1):
                def write_block(region, width, col, k, slot):
                    act.wait_ge(s_blk, k + 1)
                    dest = region[:, :, ds(col, GN)].rearrange("p s n -> p n s")
                    nc.scalar.copy(dest, ps[:, slot, 0:GN * NBLK].rearrange("p (n s) -> p n s", s=NBLK)).then_inc(s_adj, 1)

                for c in range(NCH - 1):
                    region = adj[:, COFF[c]:COFF[c] + NBLK * CH].rearrange("p (s n) -> p s n", s=NBLK)
                    with act.Fori(0, GPC // 2) as i:
                        for slot in range(2):
                            write_block(region, CH, i * (2 * GN) + slot * GN, i * 2 + (GPC * c + slot), slot)
                region = adj[:, COFF[-1]:COFF[-1] + NBLK * SW[-1]].rearrange("p (s n) -> p s n", s=NBLK)
                act.wait_ge(s_ev, 10 + NCH)
                with act.Fori(0, LASTG // 2) as i:
                    for slot in range(2):
                        write_block(region, SW[-1], i * (2 * GN) + slot * GN, i * 2 + (GPC * (NCH - 1) + slot), slot)
                write_block(region, SW[-1], GN * (LASTG - 1), NGRP - 1, 0)

                def layer(l):
                    for t in range(NUB + 1):
                        if t < NUB:
                            b0, nb = blocks_of(t)[0], len(blocks_of(t))
                            act.wait_ge(s_uf, NUB * l + t + 1)
                            nc.scalar.copy(u[0:BLK, b0:b0 + nb, 0, :], work[0:BLK, t % 3, 0:nb * D].rearrange("p (s d) -> p s d", d=D)).then_inc(s_hi, 1)
                        if t > 0:
                            b0, nb = blocks_of(t - 1)[0], len(blocks_of(t - 1))
                            act.wait_ge(s_r1, NUB * l + t)
                            nc.scalar.copy(u[0:BLK, b0:b0 + nb, 1, :], work[0:BLK, (t - 1) % 3, 0:nb * D].rearrange("p (s d) -> p s d", d=D)).then_inc(s_mid, 1)
                    for c in range(NCH):
                        act.wait_ge(s_rd, 2 * NCH * l + 2 * c + 2)
                        nc.scalar.activation(work[:, 1, 0:CW[c]], work[:, 1, 0:CW[c]], ACT.Exp).then_inc(s_exp, 1)

                with act.Fori(0, LAYERS) as l:
                    layer(l)
                for j in range(NUB):
                    b0, nb = blocks_of(j)[0], len(blocks_of(j))
                    act.wait_ge(s_var, j + 1)
                    nc.scalar.activation(rstd[0:BLK, b0:b0 + nb], mv[0:BLK, b0:b0 + nb, 1], ACT.Sqrt, bias=epst[0:BLK, 0:1]).then_inc(s_std, 1)
                with act.Fori(0, NBLK) as c:
                    act.wait_ge(s_fv, c + 1)
                    nc.scalar.activation(fst[0:BLK, 8:9], fst[0:BLK, 7:8], ACT.Sqrt, bias=epst[0:BLK, 0:1]).then_inc(s_fs, 1)
            with act.Else():
                general_act(act)

        @block.vector
        def _(dve):
            chain = [0]

            def link(ins):
                chain[0] = chain[0] + 1
                ins.then_inc(s_vch, 1)
                dve.wait_ge(s_vch, chain[0])

            def rolled(lo, hi, links, body):
                start = chain[0]
                with dve.Fori(lo, hi) as i:
                    chain[0] = (i - lo) * links + start
                    body(i)
                chain[0] = start + links * (hi - lo)

            V = nc.vector
            dve.wait_ge(s_iota, 5)
            link(V.tensor_scalar(ident[:, :], iota_f[:, :], 0.0, None, ALU.is_equal))
            dve.wait_ge(s_dst, 16)
            link(V.tensor_copy(samp[0:BLK, 0:NSMP], dstP[0:BLK, 0:SSTEP * NSMP:SSTEP]))
            for k in range(NSMP):
                V.tensor_scalar(cmp[0:BLK, k, :], thr[0:BLK, :], samp[0:BLK, k:k + 1], None, ALU.is_gt).then_inc(s_cmp, 1)
            dve.wait_ge(s_cnt, 1)
            link(V.tensor_scalar(pos[:, 0, :], ps[:, 7, 0:UB], float(SSTEP), float(-SSTEP), ALU.mult, ALU.add))
            link(V.tensor_scalar(pos[:, 0, :], pos[:, 0, :], 0.0, float(E - SSTEP), ALU.max, ALU.min))
            V.tensor_copy(idx_s[:, :], pos[:, 0, :]).then_inc(s_idxs, 1)
            link(V.tensor_scalar(baseT[:, :], baseT[:, :], 0.5, 1.0 / TPB, ALU.add, ALU.mult))
            link(V.tensor_scalar(baseT[:, :], baseT[:, :], -0.5, MAGIC, ALU.add, ALU.add))
            link(V.tensor_scalar(baseT[:, :], baseT[:, :], MAGIC, float(WBACK), ALU.subtract, ALU.subtract))
            dve.wait_ge(s_swin, 16 * UB)
            link(V.tensor_copy(swinf[:, :, :], swin[:, :, :]))
            for b in range(UB):
                link(V.tensor_scalar(junk[:, 0:SSTEP], swinf[:, b, :], thr_g[:, b:b + 1], None, ALU.is_lt, ALU.add, accum_out=pos[:, 1, b:b + 1]))
            link(V.tensor_tensor(pos[:, 2, :], pos[:, 0, :], pos[:, 1, :], ALU.add))
            link(V.tensor_scalar(pos[:, 2, :], pos[:, 2, :], float(E - WUSE), None, ALU.min))
            V.tensor_copy(idx_w[:, :], pos[:, 2, :]).then_inc(s_idxw, 1)
            dve.wait_ge(s_ev, 10)
            link(V.tensor_tensor(dlT[0:BLK, :], edgeT[0][0:BLK, :], baseT[0:BLK, :], ALU.subtract))
            link(V.memset(totals[:, :], 0.0))
            link(V.tensor_scalar(inT[0:BLK, :], dlT[0:BLK, :], 0.0, None, ALU.is_ge))
            V.scalar_tensor_tensor(baseT[0:BLK, :], dlT[0:BLK, :], float(WN), inT[0:BLK, :], ALU.is_lt, ALU.mult,
                                   accum_out=totals[0:BLK, 1:2]).then_inc(s_dl, 1)
            dve.wait_ge(s_const, 5)
            dve.wait_ge(s_bwin, 32 * UB)
            link(V.tensor_copy(swf[:, :, :], ewin[:, :, :]))
            link(V.tensor_copy(dwf[:, :, :], dwin[:, :, :]))
            link(V.tensor_scalar(hif[:, :, :], swf[:, :, :], 0.5, 1.0 / BLK, ALU.add, ALU.mult))
            link(V.tensor_scalar(hif[:, :, :], hif[:, :, :], -0.5, MAGIC, ALU.add, ALU.add))
            link(V.tensor_scalar(hif[:, :, :], hif[:, :, :], MAGIC, None, ALU.subtract))
            V.scalar_tensor_tensor(swf[:, :, :], hif[:, :, :], float(-BLK), swf[:, :, :], ALU.mult, ALU.add).then_inc(s_win, 1)
            for b in range(UB):
                link(V.tensor_scalar(dwf[:, b, :], dwf[:, b, :], thr_g[:, b:b + 1], None, ALU.subtract))
            link(V.memset(dwf[:, :, WUSE:WIN], -1.0))
            V.scalar_tensor_tensor(hif[:, :, :], dwf[:, :, :], float(NBLK), hif[:, :, :], ALU.mult, ALU.add).then_inc(s_win, 1)
            for b in range(UB):
                for k in range(BW):
                    link(V.tensor_scalar(junk[:, 0:WIN], dwf[:, b, :], float(k), None, ALU.is_equal, ALU.add, accum_out=deg[:, b, k:k + 1]))
            V.tensor_reduce(totals[:, 0:1], deg[:, :, :], AX.XY, ALU.add).then_inc(s_tot, 1)
            dve.wait_ge(s_tot, 1)
            V.memset(flagf[:, :], 0.0).then_inc(s_deg, 1)
            dve.wait_ge(s_sq, 1)
            V.reciprocal(deg[:, :, :], deg[:, :, :]).then_inc(s_dinv, 1)
            dve.wait_ge(s_ev, NJ)
            dve.wait_ge(s_win, 2)
            V.tensor_copy(flagf[:, 0:1], totals[:, 0:1]).then_inc(s_tot, 1)
            dve.wait_ge(s_totp, 1)
            link(V.tensor_scalar(flagf[0:1, 1:3], ps[0:1, 7, 8:10], float(E), None, ALU.is_equal))
            link(V.tensor_tensor(flagf[0:1, 0:1], flagf[0:1, 1:2], flagf[0:1, 2:3], ALU.mult))
            V.tensor_copy(flag[0:1, 0:1], flagf[0:1, 0:1]).then_inc(s_flag, 1)
            before = chain[0]
            dve.wait_ge(s_flag, 1)
            covered = dve.value_load(flag[0:1, 0:1], min_val=0, max_val=1)
            with dve.If(covered == 1):
                def onehots(k, slot, first):
                    if not first:
                        dve.wait_ge(s_blk, k - 1)
                    for a in range(2):
                        w = (P, QW)[a]
                        codes = sT[a][:, ds(k * 8, 8)]
                        V.tensor_tensor(hot[slot][a][:, 0:w, :], iota_v[:, 0:w, :],
                                        codes[:, None, :].broadcast_to([P, w, 8]), ALU.is_equal).then_inc(s_hot, 1)
                onehots(0, 0, True)
                onehots(1, 1, True)
                with dve.Fori(1, NGRP // 2) as i:
                    onehots(i * 2, 0, False)
                    onehots(i * 2 + 1, 1, False)
                onehots(NGRP - 1, 0, False)
                dve.wait_ge(s_adj, NGRP)
                neye = 0
                for s in range(NBLK):
                    lo, hi = s * BLK, (s + 1) * BLK
                    while lo < hi:
                        c = lo // CH
                        e = min(hi, CH * (c + 1))
                        at = COFF[c] + s * SW[c] + lo - CH * c
                        v = adj[0:BLK, at:at + e - lo]
                        V.tensor_tensor(v, v, ident[0:BLK, lo - s * BLK:e - s * BLK], ALU.add).then_inc(s_eye, 1)
                        neye += 1
                        lo = e
                dve.wait_ge(s_dinvl, 32)
                NEYE[0] = neye

                def parts(l):
                    for t in range(NUB + 2):
                        if t < NUB:
                            b0, nb = blocks_of(t)[0], len(blocks_of(t))
                            dve.wait_ge(s_w, NUB * l + t + 1)
                            if t >= 3:
                                dve.wait_ge(s_u, NUB * l + t - 2)
                            wk = work[0:BLK, t % 3, 0:nb * D].rearrange("p (s d) -> p s d", d=D)
                            V.tensor_tensor(wk, ps[0:BLK, 5 + t % 3, 0:nb * D].rearrange("p (s d) -> p s d", d=D),
                                            dinv_col[0:BLK, b0:b0 + nb, None].broadcast_to([BLK, nb, D]), ALU.mult).then_inc(s_uf, 1)
                        if 1 <= t <= NUB:
                            q = t - 1
                            b0, nb = blocks_of(q)[0], len(blocks_of(q))
                            dve.wait_ge(s_hi, NUB * l + q + 1)
                            wk = work[0:BLK, q % 3, 0:nb * D].rearrange("p (s d) -> p s d", d=D)
                            V.tensor_tensor(wk, wk, u[0:BLK, b0:b0 + nb, 0, :], ALU.subtract).then_inc(s_r1, 1)
                        if t >= 2:
                            q = t - 2
                            b0, nb = blocks_of(q)[0], len(blocks_of(q))
                            dve.wait_ge(s_mid, NUB * l + q + 1)
                            wk = work[0:BLK, q % 3, 0:nb * D].rearrange("p (s d) -> p s d", d=D)
                            V.tensor_tensor(u[0:BLK, b0:b0 + nb, 2, :], wk, u[0:BLK, b0:b0 + nb, 1, :], ALU.subtract).then_inc(s_u, 1)
                    dve.wait_ge(s_u, NUB * l + NUB)

                def post(l, c):
                    w, at = CW[c], CH * c
                    z, m = work[:, 0, 0:w], work[:, 1, 0:w]
                    h = hT[:, at:at + w]
                    b = convb[:, ds(l, 1)]
                    dve.wait_ge(s_agg, NCH * l + c + 1)
                    V.tensor_tensor(z, ps[:, c % 5, 0:w], dinv_all[:, at:at + w], ALU.mult).then_inc(s_rd, 1)
                    dve.wait_ge(s_rd, 2 * NCH * l + 2 * c + 1)
                    V.tensor_scalar(m, z, b, 0.0, ALU.add, ALU.min).then_inc(s_rd, 1)
                    dve.wait_ge(s_rd, 2 * NCH * l + 2 * c + 2)
                    link(V.tensor_scalar(z, z, b, 0.0, ALU.add, ALU.max))
                    link(V.tensor_tensor(h, h, z, ALU.add))
                    dve.wait_ge(s_exp, NCH * l + c + 1)
                    V.scalar_tensor_tensor(h, m, -1.0, h, ALU.add, ALU.add).then_inc(s_h, 1)
                    dve.wait_ge(s_h, NCH * l + c + 1)

                def layer(l):
                    parts(l)
                    dve.wait_ge(s_hs, 16 * l + 16)
                    for c in range(NCH):
                        post(l, c)
                rolled(0, LAYERS - 1, 2 * NCH, layer)
                L = LAYERS - 1
                parts(L)
                dve.wait_ge(s_hs, 16 * LAYERS)

                def relation(r):
                    link(V.scalar_tensor_tensor(relw[0:BLK, :], tyE[0:BLK, :], float(r), wE[0:BLK, :], ALU.is_equal, ALU.mult))
                    for b in range(NB):
                        s = compB[0:BLK, r * NB + b:r * NB + b + 1]
                        if r == 0:
                            link(V.tensor_scalar(coef[0:BLK, :, b], relw[0:BLK, :], s, None, ALU.mult))
                        else:
                            link(V.scalar_tensor_tensor(coef[0:BLK, :, b], relw[0:BLK, :], s, coef[0:BLK, :, b], ALU.mult, ALU.add))
                done = 0
                for c in range(NCH):
                    post(L, c)
                    if c >= 3:
                        if c == 3:
                            dve.wait_ge(s_back[1], 64)
                        for _ in range(2):
                            if done < RELS - 2 and c < NCH - 1:
                                relation(done)
                                done += 1
                dve.wait_ge(s_back[4], 16)
                dve.wait_ge(s_back[1], 64)
                link(V.tensor_tensor(xb[0:BLK], xb[0:BLK], linbB[0:BLK, None, :].broadcast_to([BLK, NBLK, D]), ALU.add))
                for t in range(NUB + 1):
                    if t < NUB:
                        b0, nb = blocks_of(t)[0], len(blocks_of(t))
                        dve.wait_ge(s_lin, t + 1)
                        y = xb[0:BLK, b0:b0 + nb, :]
                        link(V.tensor_tensor(y, ps[0:BLK, 5 + t % 3, 0:nb * D].rearrange("p (s d) -> p s d", d=D), y, ALU.add))
                        for q in range(nb):
                            link(V.bn_stats(bnst[0:BLK, q, 0:6], xb[0:BLK, b0 + q, :]))
                        for q in range(nb):
                            ins = V.bn_aggr(mv[0:BLK, b0 + q, :], bnst[0:BLK, q, 0:6])
                            ins.then_inc(s_var, 1) if q == nb - 1 else link(ins)
                        dve.wait_ge(s_var, t + 1)
                    if t > 0:
                        b0, nb = blocks_of(t - 1)[0], len(blocks_of(t - 1))
                        dve.wait_ge(s_std, t)
                        link(V.reciprocal(rstd[0:BLK, b0:b0 + nb], rstd[0:BLK, b0:b0 + nb]))
                        for q in range(b0, b0 + nb):
                            ins = V.tensor_scalar(xb[0:BLK, q, :], xb[0:BLK, q, :], mv[0:BLK, q, 0:1], rstd[0:BLK, q:q + 1], ALU.subtract, ALU.mult)
                            ins.then_inc(s_x1, 1) if q == b0 + nb - 1 else link(ins)
                dve.wait_ge(s_x1, NUB)
                dve.wait_ge(s_back[0], 64)

                def indices(c, g):
                    V.tensor_copy(idxg[0:BLK, GG * g:GG * (g + 1)], srcI[0:BLK, ds(c * TPB + GG * g, GG)]).then_inc(s_idx, 1)
                for g in range(3):
                    indices(0, g)
                while done < RELS:
                    relation(done)
                    done += 1
                dve.wait_ge(s_zero, 3)

                def moving(c, j, first):
                    if not first:
                        dve.wait_ge(s_mu, c * TPB + (j - MS + 1))
                    V.scalar_tensor_tensor(mov[0:BLK, j % MS, :, :], iota_w[0:BLK, None, :].broadcast_to([BLK, NB, WN]),
                                           dl[0:BLK, ds(c * TPB + j, 1)],
                                           coef[0:BLK, ds(c * TPB + j, 1), :].rearrange("p t b -> p (t b)")[:, :, None].broadcast_to([BLK, NB, WN]),
                                           ALU.is_equal, ALU.mult).then_inc(s_m, 1)

                def fold(c):
                    dve.wait_ge(s_mu, c * TPB + TPB)
                    link(V.tensor_tensor(acc[:, :], ps[:, 0, 0:NB * BLK], carry[:, :], ALU.add))
                    V.tensor_copy(carry[:, :], ps[:, 1, 0:NB * BLK]).then_inc(s_fold, 1)
                    dve.wait_ge(s_fold, c + 1)

                def stats(c):
                    dve.wait_ge(s_fin, c + 1)
                    yv = ystage[0:BLK, 1, :]
                    link(V.tensor_tensor(yv, ps[0:BLK, 3, 0:D], xb[0:BLK, ds(c, 1), :].rearrange("p s d -> p (s d)"), ALU.add))
                    link(V.bn_stats(fst[0:BLK, 0:6], yv))
                    V.memset(fst[0:BLK, 10:11], 0.0)
                    V.bn_aggr(fst[0:BLK, 6:8], fst[0:BLK, 0:6]).then_inc(s_fv, 1)

                def norm(c, first):
                    dve.wait_ge(s_fs, c + 1)
                    link(V.reciprocal(fst[0:BLK, 9:10], fst[0:BLK, 8:9]))
                    if not first:
                        dve.wait_ge(s_out, c * 16)
                    V.tensor_scalar(ystage[0:BLK, 0, :], ystage[0:BLK, 1, :], fst[0:BLK, 6:7], fst[0:BLK, 9:10], ALU.subtract, ALU.mult).then_inc(s_y, 1)
                    dve.wait_ge(s_y, c + 1)

                def chunk(c, head, second=False, tail=True):
                    for j in range(TPB):
                        moving(c, j, head and j < MS)
                        if j == 1 and not head:
                            fold(c - 1)
                        if j == 8 and not head:
                            dve.wait_ge(s_mu, c * TPB + 6)
                            V.tensor_tensor(aggf[:, :, :].rearrange("p b n -> p (b n)"), ps[:, 2, 0:NB * BLK], acc[:, :], ALU.add).then_inc(s_af, 1)
                        if j == 17 and not head:
                            stats(c - 1)
                        if j == 21 and not head:
                            norm(c - 1, second)
                        for g in range(3):
                            if tail and j == min(GG * g + 5, TPB - 1):
                                dve.wait_ge(s_g[g], 16 * GG * (c + 1))
                                indices(c + 1, g)
                chunk(0, True)
                chunk(1, False, second=True)
                rolled(2, NBLK - 1, 4, lambda c: chunk(c, False))
                chunk(NBLK - 1, False, tail=False)
                fold(NBLK - 1)
                V.tensor_copy(aggf[:, :, :].rearrange("p b n -> p (b n)"), acc[:, :]).then_inc(s_af, 1)
                stats(NBLK - 1)
                norm(NBLK - 1, False)
            with dve.Else():
                chain[0] = before
                general_dve(dve, link)

        @block.tensor
        def _(pe):
            T = nc.tensor
            pe.wait_ge(s_const, 5)
            pe.wait_ge(s_cmp, NSMP)
            for b in range(UB):
                for k in range(NSMP):
                    last = T.matmul(ps[:, 7, b:b + 1], cmp[0:BLK, k, P * b:P * (b + 1)], ones[0:BLK, 0:1], start=(k == 0), stop=(k == NSMP - 1))
            last.then_inc(s_cnt, 1)
            n = 0

            def job(parts):
                nonlocal n
                if n >= 7:
                    pe.wait_ge(s_ev, n - 6)
                for o0, o1, src_ap, rows in parts:
                    last = T.transpose(ps[0:src_ap.shape[1], n % 7, o0:o1], src_ap, ident[0:rows, 0:rows])
                last.then_inc(s_job, 1)
                n += 1
            pe.wait_ge(s_wl, 64)
            job([(D * l, D * (l + 1), wst[:, l, :], P) for l in range(LAYERS)])
            job([(D * l, D * (l + 1), lst[:, D * l:D * (l + 1)], P) for l in range(LAYERS + 1)])
            for a in range(4):
                if a < 3:
                    pe.wait_ge(s_rawf, 2 * a + 2)
                else:
                    pe.wait_ge(s_raw[3], 32)
                job([(P * b, P * (b + 1), rawf[a][:, b, :], P) for b in range(4)])
                job([(P * b, P * (b + 1), rawf[a][:, 4 + b, :], P) for b in range(2)]
                    + [(2 * P, 2 * P + TAILR, rawf[a][0:TAILR, 6, :], TAILR)])
            pe.wait_ge(s_x, 16)
            for c in range(NCH):
                job([(BLK * q, BLK * (q + 1), xst[0:BLK, 4 * c + q, :], BLK) for q in range(min(4, NBLK - 4 * c))])
            for a, v in enumerate((swf, hif)):
                pe.wait_ge(s_win, a + 1)
                for q in range(3):
                    job([(256 * bb + P * h, 256 * bb + P * (h + 1), v[:, 2 * q + bb, P * h:P * (h + 1)], P)
                         for bb in range(min(2, UB - 2 * q)) for h in range(2)])
            pe.wait_ge(s_ev, NJ)

            pe.wait_ge(s_tot, 2)
            pe.wait_ge(s_dl, 1)
            T.matmul(ps[0:1, 7, 8:10], onesf[:, 0:1], totals[:, 0:2], start=True, stop=True).then_inc(s_totp, 1)
            pe.wait_ge(s_flag, 1)
            covered = pe.value_load(flag[0:1, 0:1], min_val=0, max_val=1)
            with pe.If(covered == 1):
                def build(k, slot, first):
                    pe.wait_ge(s_hot, k * 2 + 2)
                    if not first:
                        pe.wait_ge(s_adj, k - 1)
                    for g in range(GRP):
                        for h in range(2):
                            last = T.matmul(ps[:, slot, QW * g:QW * (g + 1)], hot[slot][0][:, :, 2 * g + h],
                                            hot[slot][1][:, 0:QW, 2 * g + h], start=(h == 0), stop=(h == 1))
                    last.then_inc(s_blk, 1)
                build(0, 0, True)
                build(1, 1, True)
                with pe.Fori(1, NGRP // 2) as i:
                    build(i * 2, 0, False)
                    build(i * 2 + 1, 1, False)
                build(NGRP - 1, 0, False)

                pe.wait_ge(s_eye, NEYE[0])

                def layer(l, first):
                    for j in range(NUB):
                        if not first:
                            pe.wait_ge(s_h, l * NCH + (cover(j) - NCH))
                        if j >= 3:
                            pe.wait_ge(s_uf, NUB * l + j - 2)
                        for q, s in enumerate(blocks_of(j)):
                            last = T.matmul(ps[0:BLK, 5 + j % 3, D * q:D * (q + 1)], hT[:, BLK * s:BLK * (s + 1)],
                                            wT[:, ds(l, 1), :].rearrange("p l d -> p (l d)"), start=True, stop=True)
                        last.then_inc(s_w, 1)
                    for c in range(NCH):
                        if c >= 5:
                            pe.wait_ge(s_rd, 2 * NCH * l + 2 * (c - 5) + 1)
                        for s in range(NBLK):
                            if c == 0 and s % UBT == 0:
                                pe.wait_ge(s_u, NUB * l + s // UBT + 1)
                            at = COFF[c] + s * SW[c]
                            for k in range(3):
                                last = T.matmul(ps[:, c % 5, 0:CW[c]], u[0:BLK, s, k, :], adj[0:BLK, at:at + CW[c]],
                                                start=(s == 0 and k == 0), stop=(s == NBLK - 1 and k == 2))
                        last.then_inc(s_agg, 1)
                layer(0, True)
                with pe.Fori(1, LAYERS) as l:
                    layer(l, False)
                for r in range(3):
                    pe.wait_ge(s_back[r], (64, 64, 16)[r])
                for j in range(NUB):
                    pe.wait_ge(s_h, NCH * (LAYERS - 1) + cover(j))
                    if j >= 3:
                        pe.wait_ge(s_var, j - 2)
                    for q, s in enumerate(blocks_of(j)):
                        for k in range(LAYERS + 1):
                            hk = h_old[k] if k < LAYERS else hT
                            last = T.matmul(ps[0:BLK, 5 + j % 3, D * q:D * (q + 1)], hk[:, BLK * s:BLK * (s + 1)], linT[:, k, :],
                                            start=(k == 0), stop=(k == LAYERS))
                    last.then_inc(s_lin, 1)
                pe.wait_ge(s_zero, 3)
                pe.wait_ge(s_x1, NUB)
                NPREV = sum(1 for j in range(TPB) if LO[j] < 0)

                def tile(c, j):
                    if j % GG == 0:
                        pe.wait_ge(s_g[j // GG], 16 * GG * (c + 1))
                    pe.wait_ge(s_m, c * TPB + (j + 1))
                    cuts = [(2, LO[j], min(0, LO[j] + WN)), (0, max(0, LO[j]), min(BLK, LO[j] + WN)), (1, max(BLK, LO[j]), LO[j] + WN)]
                    off = {0: 0, 1: -BLK, 2: BLK}
                    for bank, a, b in cuts:
                        if a >= b:
                            continue
                        o = ps[:, bank, 0:NB * BLK].rearrange("p (b n) -> p b n", b=NB)[:, :, a + off[bank]:b + off[bank]]
                        last = T.matmul(o, gat[0:BLK, j, :], mov[0:BLK, j % MS, :, a - LO[j]:b - LO[j]], start=False, stop=False, skip_group_check=True)
                    last.then_inc(s_mu, 1)

                def finish(c):
                    pe.wait_ge(s_af, c + 1)
                    for b in range(NB):
                        last = T.matmul(ps[0:BLK, 3, 0:D], aggf[:, b, :], basesS[:, b, :], start=(b == 0), stop=(b == NB - 1))
                    last.then_inc(s_fin, 1)

                def chunk(c, head):
                    if not head:
                        pe.wait_ge(s_fold, c)
                    for bank in (2, 0, 1):
                        T.matmul(ps[:, bank, 0:NB * BLK], zeros[:, 0:P], zeros[:, 0:NB * BLK], start=True, stop=False, skip_group_check=True)
                    for j in range(TPB):
                        tile(c, j)
                        if j == 12 and not head:
                            finish(c - 1)
                chunk(0, True)
                with pe.Fori(1, NBLK) as c:
                    chunk(c, False)
                finish(NBLK - 1)
            with pe.Else():
                general_pe(pe)


NEYE = [0]

_INS = ['x', 'src', 'dst', 'edge_type_8', 'edge_weight', 'L0_gnn_conv_w', 'L0_gnn_conv_b', 'L0_gnn_lin_w',
        'L0_gnn_lin_b', 'L1_gnn_bases', 'L1_gnn_w_comp']
_OUTS = [((3125, 128), 'float32')]


def kernel(**inputs):
    import numpy as _np
    import concourse.bacc as _bacc
    from concourse import mybir as _mybir
    from concourse.bass_utils import run_bass_kernel_spmd as _run

    nc = _bacc.Bacc("TRN2", target_bir_lowering=False, num_devices=1)
    arrays, args = {}, []
    for name in _INS:
        a = _np.ascontiguousarray(inputs[name])
        arrays[f"in_{name}_dram"] = a
        args.append(nc.dram_tensor(f"in_{name}_dram", a.shape, _mybir.dt.from_np(a.dtype), kind="ExternalInput").ap())
    for i, (shape, dtype) in enumerate(_OUTS):
        dt = _mybir.dt.from_np(_np.dtype(dtype))
        args.append(nc.dram_tensor(f"out_{i}_dram", shape, dt, kind="ExternalOutput").ap())
    build_program(nc, *args)
    r = _run(nc, [arrays], core_ids=[0])
    got = tuple(r.results[0][f"out_{i}_dram"] for i in range(len(_OUTS)))
    return got[0]
```

```python
import concourse.bass as bass
from concourse import mybir
from contextlib import ExitStack


def build_program(nc, x, src, dst, etype, eweight, conv_w, conv_b, lin_w, lin_b, bases, w_comp, out):
    fp32, bf16 = mybir.dt.float32, mybir.dt.bfloat16
    i32, u32 = mybir.dt.int32, mybir.dt.uint32
    ALU = mybir.AluOpType
    ACT = mybir.ActivationFunctionType
    AX = mybir.AxisListType
    ds = bass.ds

    P = 128
    N, D = x.shape
    E = src.shape[0]
    LAYERS = conv_w.shape[0]
    RELS, NB = w_comp.shape
    BLK = 125
    NBLK = N // BLK
    TILES = E // BLK
    TPB = TILES // NBLK
    assert N == NBLK * BLK and E == TILES * BLK and TILES == TPB * NBLK
    BW = 5
    QW = BW * NBLK
    WIN = 256
    WUSE = WIN - 1
    UB = 5
    NBUK = UB * P
    SSTEP = 165
    NSMP = E // SSTEP // BLK
    GRP = 4
    GN = GRP * BW
    NGRP = -(-(N // BW) // GRP)
    CH = 480
    GPC = CH // GN
    NCH = -(-N // CH)
    LASTG = NGRP - GPC * (NCH - 1)
    CW = [CH] * (NCH - 1) + [N - CH * (NCH - 1)]
    SW = [CH] * (NCH - 1) + [LASTG * GN]
    COFF = [CH * NBLK * c for c in range(NCH)]
    ADJ = COFF[-1] + NBLK * SW[-1]
    UBT = 4
    NUB = -(-NBLK // UBT)
    WN = 48
    WBACK = 21
    LO = [BLK * j // TPB - WBACK for j in range(TPB)]
    MAGIC = 12582912.0
    EPS = 1e-5
    BIG = 6 * P
    TAILR = TILES - BIG

    ctx = ExitStack()
    with ctx:
        def sb(name, shape, dt):
            return ctx.enter_context(nc.sbuf_tensor(name, shape, dt))

        def sem(name):
            return ctx.enter_context(nc.semaphore(name))

        arena = sb("arena", [P, ADJ], bf16)
        hT = sb("hT", [P, N], fp32)
        dinv_all = sb("dinv_all", [P, N], fp32)
        u = sb("u", [P, NBLK, 3, D], bf16)
        work = sb("work", [P, 3, UBT * D], fp32)
        wT = sb("wT", [P, LAYERS, D], fp32)
        linT = sb("linT", [P, LAYERS + 1, D], fp32)
        convb = sb("convb", [P, LAYERS], fp32)
        ident = sb("ident", [P, P], fp32)
        ones = sb("ones", [P, P], bf16)
        onesf = sb("onesf", [P, 1], fp32)
        dinv_col = sb("dinv_col", [P, NBLK], fp32)
        thr_g = sb("thr_g", [P, UB], fp32)
        idx_s = sb("idx_s", [P, UB], u32)
        idx_w = sb("idx_w", [P, UB], u32)
        pos = sb("pos", [P, 3, UB], fp32)
        deg = sb("deg", [P, UB, BW], fp32)
        flag = sb("flag", [P, 1], i32)
        epst = sb("epst", [P, 1], fp32)
        compB = sb("compB", [P, RELS * NB], fp32)

        adj = arena[:, ADJ // 2:ADJ].bitcast(mybir.dt.float8e5)
        adj_codes = arena[:, ADJ // 2:ADJ].bitcast(mybir.dt.uint8)
        CODE8 = 0x48

        def carve(byte, cols, dt, size):
            return arena[:, byte // 2:(byte + cols * size) // 2].bitcast(dt)

        dstP = carve(0, TILES, i32, 4)
        thr = carve(3300 + 28, NBUK, fp32, 4)
        cmp = arena[:, 3200:3200 + UB * NBUK].rearrange("p (k g) -> p k g", k=UB)
        samp = carve(12800, 32, fp32, 4)
        swin = carve(13056, UB * SSTEP, i32, 4).rearrange("p (b e) -> p b e", b=UB)
        swinf = carve(16384, UB * SSTEP, fp32, 4).rearrange("p (b e) -> p b e", b=UB)
        EW = UB * WIN
        dwin = carve(20480, EW, i32, 4).rearrange("p (b e) -> p b e", b=UB)
        ewin = carve(25600, EW, i32, 4).rearrange("p (b e) -> p b e", b=UB)
        dwf = carve(30720, EW, fp32, 4).rearrange("p (b e) -> p b e", b=UB)
        swf = carve(35840, EW, fp32, 4).rearrange("p (b e) -> p b e", b=UB)
        hif = carve(40960, EW, fp32, 4).rearrange("p (b e) -> p b e", b=UB)
        junk = carve(46080, 1024, fp32, 4)
        RAW = 7 * BLK
        raws = [carve(72000 + 3520 * a, RAW, dt, 4).rearrange("p (b e) -> p b e", b=7)
                for a, dt in enumerate((i32, i32, i32, fp32))]
        rawf = [carve(86400 + 3520 * a, RAW, fp32, 4).rearrange("p (b e) -> p b e", b=7) for a in range(3)] + [raws[3]]
        edgeT = [carve(97280 + 3328 * a, TILES, dt, 4) for a, dt in enumerate((fp32, u32, fp32, fp32))]
        baseT = carve(110720, TILES, fp32, 4)
        dlT = carve(114048, TILES, fp32, 4)
        inT = carve(117376, TILES, fp32, 4)
        wst = carve(121600, LAYERS * D, fp32, 4).rearrange("p (l d) -> p l d", l=LAYERS)
        lst = carve(123392, (LAYERS + 1) * D, fp32, 4)
        iota_f = carve(126976, P, fp32, 4)
        xst = carve(COFF[-1] * 2, NBLK * D, fp32, 4).rearrange("p (s d) -> p s d", s=NBLK)
        SLOTS = 4
        uflat = arena[:, 50304 // 2:(50304 + 7168 + 16384) // 2]
        sT = [uflat[:, 1280 * a:1280 * (a + 1)] for a in range(2)]
        identb = arena[:, 47616 // 2:47616 // 2 + P]
        totals = carve(47872, 4, fp32, 4)
        flagf = carve(47904, 4, fp32, 4)
        most = carve(47936, 8, fp32, 4)
        OHC = P * GRP * 2
        hot = [[uflat[:, 3584 + OHC * (2 * s + a):3584 + OHC * (2 * s + a + 1)].rearrange("p (v t) -> p v t", t=8)
                for a in range(2)] for s in range(SLOTS)]
        iota_v = uflat[:, 2560:2560 + OHC].rearrange("p (v t) -> p v t", t=8)
        RB = CH * NBLK * 2
        h_old = [carve(RB * l, N, fp32, 4) for l in range(LAYERS)]
        basesS = carve(12544, NB * D, fp32, 4).rearrange("p (b d) -> p b d", b=NB)
        srcI = carve(14592, TILES, u32, 4)
        dl = carve(17920, TILES, fp32, 4)
        wE = carve(RB + 12544, TILES, fp32, 4)
        tyE = carve(RB + 15872, TILES, fp32, 4)
        linbB = carve(RB + 19200, D, fp32, 4)
        coef = carve(3 * RB, TILES * NB, fp32, 4).rearrange("p (t b) -> p t b", b=NB)
        relw = carve(3 * RB + 13312, TILES, fp32, 4)
        xb = carve(4 * RB, NBLK * D, fp32, 4).rearrange("p (s d) -> p s d", s=NBLK)
        acc = carve(4 * RB + 12800, NB * BLK, fp32, 4)
        carry = carve(4 * RB + 14848, NB * BLK, fp32, 4)
        aggf = carve(4 * RB + 16896, NB * BLK, fp32, 4).rearrange("p (b n) -> p b n", b=NB)
        bnst = carve(4 * RB + 18944, UBT * 8, fp32, 4).rearrange("p (t s) -> p t s", t=UBT)
        mv = carve(4 * RB + 19072, NBLK * 2, fp32, 4).rearrange("p (t s) -> p t s", s=2)
        rstd = carve(4 * RB + 19328, NBLK, fp32, 4)
        iota_w = carve(4 * RB + 19456, WN, fp32, 4)
        iota_wf = carve(4 * RB + 19712, P, fp32, 4)
        ystage = carve(4 * RB + 20480, 2 * D, fp32, 4).rearrange("p (s d) -> p s d", s=2)
        fst = carve(4 * RB + 21504, 16, fp32, 4)
        idxg = carve(4 * RB + 21632, TPB, u32, 4)
        gat = carve(5 * RB, TPB * D, fp32, 4).rearrange("p (j d) -> p j d", j=TPB)
        MS = 3
        mov = carve(5 * RB + 17408, MS * NB * WN, fp32, 4).rearrange("p (s b w) -> p s b w", s=MS, b=NB)
        zeros = arena[:, (5 * RB + 20480) // 2:(5 * RB + 20480) // 2 + 512]

        H4 = 12544
        g_h = [carve(H4 * l, N, fp32, 4) for l in range(LAYERS)]
        g_hs = carve(H4 * 3, N, fp32, 4)
        g_iota = carve(H4 * 4, N, fp32, 4)
        g_hot = carve(H4 * 5, N, fp32, 4)
        G0 = H4 * 6
        g_dst, g_src, g_w, g_ty = [carve(G0 + 3328 * a, TILES, dt, 4) for a, dt in enumerate((fp32, u32, fp32, fp32))]
        g_relw = carve(G0 + 4 * 3328, TILES, fp32, 4)
        g_coef = carve(G0 + 5 * 3328, TILES * NB, fp32, 4).rearrange("p (t b) -> p t b", b=NB)
        g_xb = carve(G0 + 33280, NBLK * D, fp32, 4).rearrange("p (s d) -> p s d", s=NBLK)
        g_tab = carve(G0 + 46080, NBLK * D, fp32, 4).rearrange("p (s d) -> p s d", s=NBLK)
        g_rows = carve(G0 + 58880, D, fp32, 4)
        g_linb = carve(G0 + 59392, D, fp32, 4)
        g_bases = carve(G0 + 59904, NB * D, fp32, 4).rearrange("p (b d) -> p b d", b=NB)
        g_bn = carve(G0 + 61952, 8, fp32, 4)
        g_mv = carve(G0 + 61984, NBLK * 2, fp32, 4).rearrange("p (t s) -> p t s", s=2)
        g_std = carve(G0 + 62208, 32, fp32, 4)
        g_idx1 = carve(G0 + 62336, 8, u32, 4)
        g_nop = carve(G0 + 62368, 8, fp32, 4)
        g_zero = carve(G0 + 62400, P, fp32, 4)

        table_d = nc.dram_tensor("table_scratch", [N, D], fp32, kind="Internal").ap()
        dinv_d = nc.dram_tensor("dinv_scratch", [NBUK * BW], fp32, kind="Internal").ap()
        edge_d = [nc.dram_tensor(f"edge_scratch{a}", [BLK, TILES], dt, kind="Internal").ap()
                  for a, dt in enumerate((fp32, u32, fp32, fp32, fp32))]
        h_d = [nc.dram_tensor(f"h_scratch{l}", [P, N], fp32, kind="Internal").ap() for l in range(LAYERS)]
        x1_d = nc.dram_tensor("x1_scratch", [N, D], fp32, kind="Internal").ap()

        ps = ctx.enter_context(nc.psum_tensor("ps", [P, 8, 512], fp32))

        s_dst = sem("dst_loaded")
        s_raw = [sem(f"edges_loaded{a}") for a in range(4)]
        s_x = sem("x_loaded")
        s_wl = sem("weights_loaded")
        s_iota = sem("iotas_made")
        s_const = sem("constants_made")
        s_cmp = sem("samples_compared")
        s_cnt = sem("samples_counted")
        s_idxs = sem("sample_windows_known")
        s_swin = sem("sample_windows_loaded")
        s_idxw = sem("bucket_windows_known")
        s_bwin = sem("bucket_windows_loaded")
        s_rawf = sem("edges_as_floats")
        s_job = sem("transposed")
        s_ev = sem("transposes_copied")
        s_win = sem("window_codes_ready")
        s_deg = sem("degrees_ready")
        s_sq = sem("sqrt_ready")
        s_dinv = sem("dinv_ready")
        s_dinvd = sem("dinv_stored")
        s_dinvl = sem("dinv_loaded")
        s_dl = sem("window_places_ready")
        s_edst = sem("edges_stored")
        s_tot = sem("totals_ready")
        s_totp = sem("totals_summed")
        s_hot = sem("onehots_ready")
        s_blk = sem("bucket_blocks_ready")
        s_adj = sem("adjacency_written")
        s_most = sem("largest_counts_known")
        s_w = sem("hw_ready")
        s_uf = sem("u_scaled")
        s_hi = sem("u_part0")
        s_r1 = sem("u_rest1")
        s_mid = sem("u_part1")
        s_u = sem("u_ready")
        s_agg = sem("aggregated")
        s_rd = sem("aggregate_read")
        s_exp = sem("exp_ready")
        s_h = sem("h_ready")
        s_hs = sem("h_stored")
        s_back = [sem(f"reloaded{r}") for r in range(6)]
        s_xb = sem("x_plus_bias")
        s_lin = sem("lin_ready")
        s_var = sem("variance_ready")
        s_std = sem("std_ready")
        s_x1 = sem("x1_ready")
        s_x1d = sem("x1_stored")
        s_idx = sem("indices_ready")
        s_g = [sem(f"gathered{g}") for g in range(3)]
        s_m = sem("moving_ready")
        s_mu = sem("tile_done")
        s_zero = sem("zeros_made")
        s_fold = sem("chunk_folded")
        s_af = sem("chunk_sum_ready")
        s_fin = sem("chunk_transformed")
        s_fv = sem("chunk_variance")
        s_fs = sem("chunk_std")
        s_y = sem("chunk_normalised")
        s_out = sem("chunk_stored")
        s_flag = sem("flag_ready")
        s_vch = sem("dve_chain")
        s_ach = sem("act_chain")
        s_pch = sem("pool_chain")

        e_ld = sem("g_loaded")
        e_io = sem("g_constants_made")
        e_idx = sem("g_indices_ready")
        e_hot = sem("g_onehots_ready")
        e_ga = [sem(f"g_rows_gathered{p}") for p in range(LAYERS + NB)]
        e_mm = sem("g_tile_done")
        e_sq = sem("g_sqrt_ready")
        e_dinv = sem("g_dinv_ready")
        e_hs = sem("g_scaled_h_ready")
        e_tab = sem("g_table_blocks_made")
        e_tc = sem("g_table_blocks_copied")
        e_td = sem("g_table_stored")
        e_min = sem("g_min_ready")
        e_exp = sem("g_exp_ready")
        e_h = sem("g_h_ready")
        e_lin = sem("g_product_ready")
        e_lc = sem("g_product_taken")
        e_var = sem("g_variance_ready")
        e_std = sem("g_std_ready")
        e_x1 = sem("g_x1_ready")
        e_x1d = sem("g_x1_stored")
        e_agg = sem("g_aggregate_copied")
        e_y = sem("g_result_ready")
        e_out = sem("g_result_stored")
        e_nop = sem("g_wait_taken")

        GG = TPB // 3
        NJ = 2 + 8 + NCH + 6

        def cover(j):
            need = min(N, (j + 1) * UBT * BLK)
            return -(-need // CH)

        def blocks_of(j):
            return range(UBT * j, min(NBLK, UBT * (j + 1)))

        def agg_bank(l, c):
            return c % 3 if l == 0 else c % 5

        block = ctx.enter_context(nc.Block())

        GC = UBT * BLK
        GW = [min(N, GC * (c + 1)) - GC * c for c in range(NUB)]
        PASSES = 1 + LAYERS + NB

        def general_sp(sp):
            sp.wait_ge(s_x1d, 16 * NUB)
            sp.wait_ge(s_zero, 3)
            sp.dma_start(hT[:, :], h_d[0]).then_inc(e_ld, 16)
            for t, a in ((g_dst, 4), (g_src, 1), (g_w, 3), (g_ty, 2)):
                sp.dma_start(t[0:BLK], edge_d[a]).then_inc(e_ld, 16)
            sp.dma_start(g_bases[:, :, :], bases.rearrange("b i o -> i b o")).then_inc(e_ld, 16)
            sp.dma_start(g_linb[:, :], lin_b.rearrange("(o d) -> o d", o=1).broadcast_to([P, D])).then_inc(e_ld, 16)
            sp.dma_start(g_xb[0:BLK], x.rearrange("(s p) d -> p s d", p=BLK)).then_inc(e_ld, 16)
            for l in range(LAYERS):
                sp.wait_ge(e_tc, NUB * (l + 1))
                sp.dma_start(table_d.rearrange("(s p) d -> p s d", p=BLK), g_tab[0:BLK]).then_inc(e_td, 16)
            sp.wait_ge(e_x1, 1)
            sp.dma_start(x1_d.rearrange("(s p) d -> p s d", p=BLK), g_xb[0:BLK]).then_inc(e_x1d, 16)
            sp.wait_ge(e_y, 1)
            sp.dma_start(out.rearrange("(s p) d -> p s d", p=BLK), g_tab[0:BLK]).then_inc(e_out, 16)
            sp.wait_ge(e_out, 16)

        def general_pool(pool):
            pool.wait_ge(s_x1d, 16 * NUB)
            nc.gpsimd.iota(g_iota[:, :], pattern=[[1, N]], base=0, channel_multiplier=0, allow_small_or_imprecise_dtypes=True).then_inc(e_io, 1)
            nc.gpsimd.memset(g_rows[:, :], 1.0).then_inc(e_io, 1)
            nc.gpsimd.memset(g_zero[:, :], 0.0).then_inc(e_io, 1)
            nc.gpsimd.memset(g_nop[:, :], 0.0).then_inc(e_nop, 1)
            for p in range(1, PASSES):
                table = table_d if p <= LAYERS else x1_d
                if p <= LAYERS:
                    pool.wait_ge(e_td, 16 * p)
                else:
                    pool.wait_ge(e_x1d, 16)
                with pool.Fori(0, TILES) as t:
                    pool.wait_ge(e_idx, t + (TILES * (p - 1) + 1))
                    pool.wait_ge(e_nop, t + (TILES * (p - 1) + 1))
                    nc.gpsimd.tensor_tensor(g_nop[:, 0:1], epst[:, 0:1], epst[:, 0:1], ALU.add).then_inc(e_nop, 1)
                    nc.gpsimd.indirect_dma_start(out=g_rows[0:BLK, :], out_offset=None, in_=table,
                                                 in_offset=bass.IndirectOffsetOnAxis(ap=g_idx1[0:BLK, 0:1], axis=0)).then_inc(e_ga[p - 1], 16)

        def general_act(act):
            act.wait_ge(e_mm, TILES + 1)
            for c in range(NUB):
                ins = nc.scalar.activation(dinv_all[:, GC * c:GC * c + GW[c]], ps[:, c, 0:GW[c]], ACT.Sqrt, bias=onesf[:, 0:1])
                ins.then_inc(e_sq, 1)
            for l in range(LAYERS):
                for c in range(NUB):
                    act.wait_ge(e_min, NUB * l + c + 1)
                    nc.scalar.activation(work[:, 1, 0:GW[c]], work[:, 1, 0:GW[c]], ACT.Exp).then_inc(e_exp, 1)
            for r in range(2):
                act.wait_ge(e_var, r + 1)
                nc.scalar.activation(g_std[0:BLK, 0:NBLK], g_mv[0:BLK, :, 1], ACT.Sqrt, bias=epst[0:BLK, 0:1]).then_inc(e_std, 1)

        def general_dve(dve, link):
            V = nc.vector
            dve.wait_ge(e_ld, 16 * 8)
            dve.wait_ge(e_io, 3)
            for r in range(RELS):
                link(V.scalar_tensor_tensor(g_relw[0:BLK, :], g_ty[0:BLK, :], float(r), g_w[0:BLK, :], ALU.is_equal, ALU.mult))
                for b in range(NB):
                    k = compB[0:BLK, r * NB + b:r * NB + b + 1]
                    if r == 0:
                        link(V.tensor_scalar(g_coef[0:BLK, :, b], g_relw[0:BLK, :], k, None, ALU.mult))
                    else:
                        link(V.scalar_tensor_tensor(g_coef[0:BLK, :, b], g_relw[0:BLK, :], k, g_coef[0:BLK, :, b], ALU.mult, ALU.add))

            def onehots(p):
                with dve.Fori(0, TILES) as t:
                    dve.wait_ge(e_mm, t + ((TILES + 1) * p + 1))
                    if p > 0:
                        V.tensor_copy(g_idx1[0:BLK, 0:1], g_src[0:BLK, ds(t, 1)]).then_inc(e_idx, 1)
                    if p <= LAYERS:
                        V.tensor_scalar(g_hot[0:BLK, :], g_iota[0:BLK, :], g_dst[0:BLK, ds(t, 1)], None, ALU.is_equal).then_inc(e_hot, 1)
                    else:
                        co = g_coef[0:BLK, ds(t, 1), p - 1 - LAYERS]
                        V.tensor_scalar(g_hot[0:BLK, :], g_iota[0:BLK, :], g_dst[0:BLK, ds(t, 1)], co, ALU.is_equal, ALU.mult).then_inc(e_hot, 1)
                dve.wait_ge(e_mm, (TILES + 1) * (p + 1))

            onehots(0)
            dve.wait_ge(e_sq, NUB)
            V.reciprocal(dinv_all[:, :], dinv_all[:, :]).then_inc(e_dinv, 1)
            dve.wait_ge(e_dinv, 1)
            for l in range(LAYERS):
                link(V.tensor_copy(g_h[l][:, :], hT[:, :]))
                V.tensor_tensor(g_hs[:, :], hT[:, :], dinv_all[:, :], ALU.mult).then_inc(e_hs, 1)
                for j in range(NUB):
                    b0, nb = blocks_of(j)[0], len(blocks_of(j))
                    dve.wait_ge(e_tab, NUB * l + j + 1)
                    if l > 0 and j == 0:
                        dve.wait_ge(e_td, 16 * l)
                    V.tensor_copy(g_tab[0:BLK, b0:b0 + nb, :], ps[0:BLK, 7, 0:nb * D].rearrange("p (s d) -> p s d", d=D)).then_inc(e_tc, 1)
                onehots(1 + l)
                for c in range(NUB):
                    w, at = GW[c], GC * c
                    z, m, h = work[:, 0, 0:w], work[:, 1, 0:w], hT[:, at:at + w]
                    bias = convb[:, l:l + 1]
                    link(V.tensor_tensor(z, ps[:, c, 0:w], dinv_all[:, at:at + w], ALU.mult))
                    V.tensor_scalar(m, z, bias, 0.0, ALU.add, ALU.min).then_inc(e_min, 1)
                    link(V.tensor_scalar(z, z, bias, 0.0, ALU.add, ALU.max))
                    link(V.tensor_tensor(h, h, z, ALU.add))
                    dve.wait_ge(e_exp, NUB * l + c + 1)
                    V.scalar_tensor_tensor(h, m, -1.0, h, ALU.add, ALU.add).then_inc(e_h, 1)
                    dve.wait_ge(e_h, NUB * l + c + 1)
            link(V.tensor_tensor(g_xb[0:BLK], g_xb[0:BLK], g_linb[0:BLK, None, :].broadcast_to([BLK, NBLK, D]), ALU.add))

            def take(n, j, into):
                b0, nb = blocks_of(j)[0], len(blocks_of(j))
                dve.wait_ge(e_lin, NUB * n + j + 1)
                o = into[0:BLK, b0:b0 + nb, :]
                V.tensor_tensor(o, ps[0:BLK, 7, 0:nb * D].rearrange("p (s d) -> p s d", d=D), o, ALU.add).then_inc(e_lc, 1)

            def norm(r, v):
                for s in range(NBLK):
                    link(V.bn_stats(g_bn[0:BLK, 0:6], v[0:BLK, s, :]))
                    ins = V.bn_aggr(g_mv[0:BLK, s, :], g_bn[0:BLK, 0:6])
                    ins.then_inc(e_var, 1) if s == NBLK - 1 else link(ins)
                dve.wait_ge(e_std, r + 1)
                link(V.reciprocal(g_std[0:BLK, 0:NBLK], g_std[0:BLK, 0:NBLK]))
                for s in range(NBLK):
                    ins = V.tensor_scalar(v[0:BLK, s, :], v[0:BLK, s, :], g_mv[0:BLK, s, 0:1], g_std[0:BLK, s:s + 1], ALU.subtract, ALU.mult)
                    ins.then_inc((e_x1, e_y)[r], 1) if s == NBLK - 1 else link(ins)

            for j in range(NUB):
                take(0, j, g_xb)
            dve.wait_ge(e_lc, NUB)
            norm(0, g_xb)
            dve.wait_ge(e_x1, 1)
            dve.wait_ge(e_td, 16 * LAYERS)
            link(V.tensor_copy(g_tab[0:BLK], g_xb[0:BLK]))
            for b in range(NB):
                onehots(1 + LAYERS + b)
                for c in range(NUB):
                    ins = V.tensor_copy(g_hs[:, GC * c:GC * c + GW[c]], ps[:, c, 0:GW[c]])
                    ins.then_inc(e_agg, 1)
                for j in range(NUB):
                    take(1 + b, j, g_tab)
            dve.wait_ge(e_lc, NUB * (1 + NB))
            norm(1, g_tab)

        def general_pe(pe):
            T = nc.tensor
            pe.wait_ge(e_io, 3)
            pe.wait_ge(e_ld, 16 * 8)

            def tiles(p):
                with pe.Fori(0, TILES) as t:
                    if p > 0:
                        pe.wait_ge(e_ga[p - 1], t * 16 + 16)
                    pe.wait_ge(e_hot, t + (TILES * p + 1))
                    for c in range(NUB):
                        last = T.matmul(ps[:, c, 0:GW[c]], g_rows[0:BLK, :], g_hot[0:BLK, GC * c:GC * c + GW[c]],
                                        start=False, stop=False, skip_group_check=True)
                    last.then_inc(e_mm, 1)

            def clear():
                for c in range(NUB):
                    last = T.matmul(ps[:, c, 0:GW[c]], g_zero[:, :], g_iota[:, 0:GW[c]],
                                    start=True, stop=False, skip_group_check=True)
                last.then_inc(e_mm, 1)
            clear()
            tiles(0)
            for l in range(LAYERS):
                pe.wait_ge(e_hs, l + 1)
                for j in range(NUB):
                    if l + j > 0:
                        pe.wait_ge(e_tc, NUB * l + j)
                    for q, s in enumerate(blocks_of(j)):
                        last = T.matmul(ps[0:BLK, 7, D * q:D * (q + 1)], g_hs[:, BLK * s:BLK * (s + 1)], wT[:, l, :], start=True, stop=True)
                    last.then_inc(e_tab, 1)
                for c in range(NUB):
                    last = T.matmul(ps[:, c, 0:GW[c]], wT[:, l, :], g_hs[:, GC * c:GC * c + GW[c]],
                                    start=True, stop=False, skip_group_check=True)
                last.then_inc(e_mm, 1)
                tiles(1 + l)
                pe.wait_ge(e_h, NUB * (l + 1))
            for j in range(NUB):
                if j == 0:
                    pe.wait_ge(e_tc, NUB * LAYERS)
                else:
                    pe.wait_ge(e_lc, j)
                for q, s in enumerate(blocks_of(j)):
                    for k in range(LAYERS + 1):
                        hk = g_h[k] if k < LAYERS else hT
                        last = T.matmul(ps[0:BLK, 7, D * q:D * (q + 1)], hk[:, BLK * s:BLK * (s + 1)], linT[:, k, :],
                                        start=(k == 0), stop=(k == LAYERS))
                last.then_inc(e_lin, 1)
            for b in range(NB):
                if b > 0:
                    pe.wait_ge(e_agg, NUB * b)
                clear()
                tiles(1 + LAYERS + b)
                pe.wait_ge(e_agg, NUB * (b + 1))
                for j in range(NUB):
                    pe.wait_ge(e_lc, NUB * (1 + b) + j)
                    for q, s in enumerate(blocks_of(j)):
                        last = T.matmul(ps[0:BLK, 7, D * q:D * (q + 1)], g_hs[:, BLK * s:BLK * (s + 1)], g_bases[:, b, :], start=True, stop=True)
                    last.then_inc(e_lin, 1)

        @block.sync
        def _(sp):
            sp.dma_start(dstP[0:BLK, :], dst.rearrange("(p t) -> p t", t=TILES)).then_inc(s_dst, 16)
            for a, arr in enumerate((dst, src, etype, eweight)):
                sp.dma_start(raws[a][:, 0:6, :], arr[0:BIG * BLK].rearrange("(b p e) -> p b e", p=P, e=BLK)).then_inc(s_raw[a], 16)
                sp.dma_start(raws[a][0:TAILR, 6, :], arr[BIG * BLK:E].rearrange("(p e) -> p e", e=BLK)).then_inc(s_raw[a], 16)
            sp.dma_start(wst, conv_w.rearrange("l o i -> o l i")).then_inc(s_wl, 16)
            sp.dma_start(lst, lin_w).then_inc(s_wl, 16)
            with nc.allow_non_contiguous_dma(reason="three short columns"):
                sp.dma_start(convb[:, :], conv_b.rearrange("l d -> d l")).then_inc(s_wl, 16)
            sp.dma_start(compB[:, :], w_comp.rearrange("(o r) b -> o (r b)", o=1).broadcast_to([P, RELS * NB])).then_inc(s_wl, 16)
            sp.dma_start(xst[0:BLK], x.rearrange("(s p) d -> p s d", p=BLK)).then_inc(s_x, 16)
            sp.wait_ge(s_dinv, 1)
            sp.dma_start(dinv_d.rearrange("(b p k) -> p b k", p=P, k=BW), deg[:, :, :]).then_inc(s_dinvd, 16)
            sp.wait_ge(s_dl, 1)
            for a, t in enumerate((dlT, edgeT[1], edgeT[2], edgeT[3], edgeT[0])):
                sp.dma_start(edge_d[a], t[0:BLK, :]).then_inc(s_edst, 16)
            sp.wait_ge(s_dinvd, 16)
            with nc.allow_non_contiguous_dma(reason="a column per row block"):
                sp.dma_start(dinv_col[0:BLK, :], dinv_d[0:N].rearrange("(s p) -> p s", p=BLK)).then_inc(s_dinvl, 16)
            sp.dma_start(dinv_all[:, :], dinv_d[0:N].rearrange("(o n) -> o n", o=1).broadcast_to([P, N])).then_inc(s_dinvl, 16)
            sp.wait_ge(s_ev, 10 + NCH)
            sp.dma_start(h_d[0], hT[:, :]).then_inc(s_hs, 16)
            for l in range(LAYERS - 1):
                sp.wait_ge(s_h, NCH * (l + 1))
                sp.dma_start(h_d[l + 1], hT[:, :]).then_inc(s_hs, 16)
            A0 = NCH * (LAYERS - 1)
            sp.wait_ge(s_edst, 80)
            sp.wait_ge(s_hs, 16 * LAYERS)
            sp.dma_start(h_old[0], h_d[0]).then_inc(s_back[0], 16)
            sp.dma_start(srcI[0:BLK], edge_d[1]).then_inc(s_back[0], 16)
            sp.dma_start(dl[0:BLK], edge_d[0]).then_inc(s_back[0], 16)
            sp.dma_start(basesS[:, :, :], bases.rearrange("b i o -> i b o")).then_inc(s_back[0], 16)
            sp.dma_start(h_old[1], h_d[1]).then_inc(s_back[1], 16)
            sp.dma_start(wE[0:BLK], edge_d[3]).then_inc(s_back[1], 16)
            sp.dma_start(tyE[0:BLK], edge_d[2]).then_inc(s_back[1], 16)
            sp.dma_start(linbB[:, :], lin_b.rearrange("(o d) -> o d", o=1).broadcast_to([P, D])).then_inc(s_back[1], 16)
            sp.dma_start(h_old[2], h_d[2]).then_inc(s_back[2], 16)
            sp.wait_ge(s_agg, A0 + 3)
            sp.dma_start(xb[0:BLK], x.rearrange("(s p) d -> p s d", p=BLK)).then_inc(s_back[4], 16)
            for j in range(NUB):
                b0, b1 = blocks_of(j)[0], blocks_of(j)[-1] + 1
                sp.wait_ge(s_x1, j + 1)
                sp.dma_start(x1_d[b0 * BLK:b1 * BLK, :].rearrange("(s p) d -> p s d", p=BLK), xb[0:BLK, b0:b1, :]).then_inc(s_x1d, 16)
            out_v = out.rearrange("(s p) d -> s p d", p=BLK)
            sp.wait_ge(s_flag, 1)
            covered = sp.value_load(flag[0:1, 0:1], min_val=0, max_val=1)
            with sp.If(covered == 1):
                with sp.Fori(0, NBLK) as c:
                    sp.wait_ge(s_y, c + 1)
                    sp.dma_start(out_v[ds(c, 1), :, :].rearrange("s p d -> (s p) d"), ystage[0:BLK, 0, :]).then_inc(s_out, 16)
                sp.wait_ge(s_out, 16 * NBLK)
            with sp.Else():
                general_sp(sp)

        @block.gpsimd
        def _(pool):
            nc.gpsimd.iota(thr[:, :], pattern=[[BW, NBUK]], base=0, channel_multiplier=0, allow_small_or_imprecise_dtypes=True).then_inc(s_iota, 1)
            nc.gpsimd.iota(thr_g[:, :], pattern=[[BW * P, UB]], base=0, channel_multiplier=BW, allow_small_or_imprecise_dtypes=True).then_inc(s_iota, 1)
            nc.gpsimd.iota(iota_f[:, :], pattern=[[1, P]], base=0, channel_multiplier=-1, allow_small_or_imprecise_dtypes=True).then_inc(s_iota, 1)
            nc.gpsimd.iota(iota_v[:, :, :], pattern=[[1, P], [0, 8]], base=0, channel_multiplier=0, allow_small_or_imprecise_dtypes=True).then_inc(s_iota, 1)
            nc.gpsimd.iota(baseT[:, :], pattern=[[BLK, TILES]], base=0, channel_multiplier=0, allow_small_or_imprecise_dtypes=True).then_inc(s_iota, 1)
            nc.gpsimd.memset(ones[:, :], 1.0).then_inc(s_const, 1)
            nc.gpsimd.memset(onesf[:, :], 1.0).then_inc(s_const, 1)
            nc.gpsimd.memset(epst[:, :], EPS).then_inc(s_const, 1)
            nc.gpsimd.memset(dwin[:, :, WUSE:WIN], 0).then_inc(s_const, 1)
            nc.gpsimd.memset(ewin[:, :, WUSE:WIN], 0).then_inc(s_const, 1)
            edges_of = [a.rearrange("(n o) -> n o", o=1) for a in (dst, src)]
            pool.wait_ge(s_idxs, 1)
            for b in range(UB):
                nc.gpsimd.indirect_dma_start(out=swin[:, b, :], out_offset=None, in_=edges_of[0],
                                             in_offset=bass.IndirectOffsetOnAxis(ap=idx_s[:, b:b + 1], axis=0)).then_inc(s_swin, 16)
            pool.wait_ge(s_idxw, 1)
            for b in range(UB):
                for a, win in enumerate((dwin, ewin)):
                    nc.gpsimd.indirect_dma_start(out=win[:, b, 0:WUSE], out_offset=None, in_=edges_of[a],
                                                 in_offset=bass.IndirectOffsetOnAxis(ap=idx_w[:, b:b + 1], axis=0)).then_inc(s_bwin, 16)
            for t in range(NUB + 1):
                if t < NUB:
                    b0, nb = blocks_of(t)[0], len(blocks_of(t))
                    pool.wait_ge(s_hi, t + 1)
                    wk = work[0:BLK, t % 3, 0:nb * D].rearrange("p (s d) -> p s d", d=D)
                    nc.gpsimd.tensor_tensor(wk, wk, u[0:BLK, b0:b0 + nb, 0, :], ALU.subtract).then_inc(s_r1, 1)
                if t >= 1:
                    b0, nb = blocks_of(t - 1)[0], len(blocks_of(t - 1))
                    pool.wait_ge(s_mid, t)
                    wk = work[0:BLK, (t - 1) % 3, 0:nb * D].rearrange("p (s d) -> p s d", d=D)
                    nc.gpsimd.tensor_tensor(u[0:BLK, b0:b0 + nb, 2, :], wk, u[0:BLK, b0:b0 + nb, 1, :], ALU.subtract).then_inc(s_u, 1)
            pool.wait_ge(s_agg, NCH * (LAYERS - 1) + 5)
            nc.gpsimd.iota(iota_w[:, :], pattern=[[1, WN]], base=0, channel_multiplier=0, allow_small_or_imprecise_dtypes=True).then_inc(s_zero, 1)
            nc.gpsimd.memset(carry[:, :], 0.0).then_inc(s_zero, 1)
            pool.wait_ge(s_agg, NCH * (LAYERS - 1) + 6)
            nc.gpsimd.memset(zeros[:, :], 0.0).then_inc(s_zero, 1)

            pool.wait_ge(s_flag, 1)
            covered = pool.value_load(flag[0:1, 0:1], min_val=0, max_val=1)
            with pool.If(covered == 1):
                def gathers(c, first):
                    for g in range(3):
                        pool.wait_ge(s_idx, 3 * c + g + 1)
                        if not first:
                            pool.wait_ge(s_mu, TPB * c - TPB + GG * (g + 1))
                        pool.wait_ge(s_x1d, 16 * NUB)
                        if not first or g:
                            pool.wait_ge(s_pch, c * 3 + g)
                        nc.gpsimd.tensor_tensor(fst[:, 12:13], epst[:, 0:1], epst[:, 0:1], ALU.add).then_inc(s_pch, 1)
                        for j in range(GG * g, GG * (g + 1)):
                            nc.gpsimd.indirect_dma_start(out=gat[0:BLK, j, :], out_offset=None, in_=x1_d,
                                                         in_offset=bass.IndirectOffsetOnAxis(ap=idxg[0:BLK, j:j + 1], axis=0)).then_inc(s_g[g], 16)
                gathers(0, True)
                with pool.Fori(1, NBLK) as c:
                    gathers(c, False)
            with pool.Else():
                general_pool(pool)

        @block.scalar
        def _(act):
            for a in range(3):
                act.wait_ge(s_raw[a], 32)
                nc.scalar.copy(rawf[a][:, 0:6, :], raws[a][:, 0:6, :]).then_inc(s_rawf, 1)
                nc.scalar.copy(rawf[a][0:TAILR, 6, :], raws[a][0:TAILR, 6, :]).then_inc(s_rawf, 1)
            n = 0

            def take(dest, rows, cols):
                nonlocal n
                act.wait_ge(s_job, n + 1)
                nc.scalar.copy(dest, ps[0:rows, n % 7, 0:cols]).then_inc(s_ev, 1)
                n += 1
            take(wT[:, :, :].rearrange("p l d -> p (l d)"), P, LAYERS * D)
            take(linT[:, :, :].rearrange("p l d -> p (l d)"), P, (LAYERS + 1) * D)
            for a in range(4):
                take(edgeT[a][0:BLK, 0:512], BLK, 512)
                take(edgeT[a][0:BLK, 512:TILES], BLK, TILES - 512)
            for c in range(NCH):
                w = min(N, 500 * (c + 1)) - 500 * c
                take(hT[:, 500 * c:500 * c + w], P, w)
            act.wait_ge(s_deg, 1)
            nc.scalar.activation(deg[:, :, :], deg[:, :, :], ACT.Sqrt, bias=onesf[:, 0:1]).then_inc(s_sq, 1)
            for a in range(2):
                for q in range(3):
                    nb = min(2, UB - 2 * q)
                    o = sT[a].rearrange("p (b g h) -> p b h g", b=UB, h=2)[:, 2 * q:2 * q + nb, :, :]
                    act.wait_ge(s_job, n + 1)
                    for bb in range(nb):
                        ins = nc.scalar.copy(o[:, bb, :, :], ps[:, n % 7, 256 * bb:256 * bb + 256].rearrange("p (h g) -> p h g", h=2))
                        if bb == nb - 1:
                            ins.then_inc(s_ev, 1)
                        else:
                            ins.then_inc(s_ach, 1)
                    n += 1
            act.wait_ge(s_edst, 80)
            act.wait_ge(s_tot, 2)

            act.wait_ge(s_ev, NJ)

            def write_block(c, i, slot):
                region = adj[:, COFF[c]:COFF[c] + NBLK * SW[c]].rearrange("p (s n) -> p s n", s=NBLK)
                k = GPC * c + 2 * i + slot
                act.wait_ge(s_blk, k + 1)
                at = i * (2 * GN) + slot * GN
                dest = region[:, :, at:at + GN].rearrange("p s n -> p n s")
                nc.scalar.copy(dest, ps[:, 3 + k % SLOTS, 0:GN * NBLK].rearrange("p (n s) -> p n s", s=NBLK), saturate=False).then_inc(s_adj, 1)

            def parts(l, t):
                if t < NUB:
                    b0, nb = blocks_of(t)[0], len(blocks_of(t))
                    act.wait_ge(s_uf, NUB * l + t + 1)
                    nc.scalar.copy(u[0:BLK, b0:b0 + nb, 0, :], work[0:BLK, t % 3, 0:nb * D].rearrange("p (s d) -> p s d", d=D)).then_inc(s_hi, 1)
                if 0 < t <= NUB:
                    b0, nb = blocks_of(t - 1)[0], len(blocks_of(t - 1))
                    act.wait_ge(s_r1, NUB * l + t)
                    nc.scalar.copy(u[0:BLK, b0:b0 + nb, 1, :], work[0:BLK, (t - 1) % 3, 0:nb * D].rearrange("p (s d) -> p s d", d=D)).then_inc(s_mid, 1)

            def exps(l, c):
                act.wait_ge(s_rd, 2 * NCH * l + 2 * c + 2)
                nc.scalar.activation(work[:, 1, 0:CW[c]], work[:, 1, 0:CW[c]], ACT.Exp).then_inc(s_exp, 1)

            for i in range(GPC // 2):
                for slot in range(2):
                    write_block(0, i, slot)
                if i >= 1:
                    parts(0, i - 1)
            for c in range(1, NCH):
                for slot in range(2):
                    write_block(c, 0, slot)
                if c >= 2:
                    exps(0, c - 2)
                for i in range(1, (GPC if c < NCH - 1 else LASTG) // 2):
                    for slot in range(2):
                        write_block(c, i, slot)
            write_block(NCH - 1, LASTG // 2, 0)
            for c in (NCH - 2, NCH - 1):
                exps(0, c)
            with act.Fori(1, LAYERS) as l:
                for t in range(NUB + 1):
                    parts(l, t)
                for c in range(NCH):
                    exps(l, c)
            for j in range(NUB):
                b0, nb = blocks_of(j)[0], len(blocks_of(j))
                act.wait_ge(s_var, j + 1)
                nc.scalar.activation(rstd[0:BLK, b0:b0 + nb], mv[0:BLK, b0:b0 + nb, 1], ACT.Sqrt, bias=epst[0:BLK, 0:1]).then_inc(s_std, 1)
            act.wait_ge(s_flag, 1)
            covered = act.value_load(flag[0:1, 0:1], min_val=0, max_val=1)
            with act.If(covered == 1):
                with act.Fori(0, NBLK) as c:
                    act.wait_ge(s_fv, c + 1)
                    nc.scalar.activation(fst[0:BLK, 8:9], fst[0:BLK, 7:8], ACT.Sqrt, bias=epst[0:BLK, 0:1]).then_inc(s_fs, 1)
            with act.Else():
                general_act(act)

        @block.vector
        def _(dve):
            chain = [0]

            def link(ins):
                chain[0] = chain[0] + 1
                ins.then_inc(s_vch, 1)
                dve.wait_ge(s_vch, chain[0])

            def rolled(lo, hi, links, body):
                start = chain[0]
                with dve.Fori(lo, hi) as i:
                    chain[0] = (i - lo) * links + start
                    body(i)
                chain[0] = start + links * (hi - lo)

            V = nc.vector
            dve.wait_ge(s_iota, 5)
            link(V.tensor_scalar(ident[:, :], iota_f[:, :], 0.0, None, ALU.is_equal))
            link(V.tensor_copy(identb[:, :], ident[:, :]))
            dve.wait_ge(s_dst, 16)
            link(V.tensor_copy(samp[0:BLK, 0:NSMP], dstP[0:BLK, 0:SSTEP * NSMP:SSTEP]))
            for k in range(NSMP):
                V.tensor_scalar(cmp[0:BLK, k, :], thr[0:BLK, :], samp[0:BLK, k:k + 1], None, ALU.is_gt).then_inc(s_cmp, 1)
            dve.wait_ge(s_cnt, 1)
            link(V.tensor_scalar(pos[:, 0, :], ps[:, 7, 0:UB], float(SSTEP), float(-SSTEP), ALU.mult, ALU.add))
            link(V.tensor_scalar(pos[:, 0, :], pos[:, 0, :], 0.0, float(E - SSTEP), ALU.max, ALU.min))
            V.tensor_copy(idx_s[:, :], pos[:, 0, :]).then_inc(s_idxs, 1)
            link(V.tensor_scalar(baseT[:, :], baseT[:, :], 0.5, 1.0 / TPB, ALU.add, ALU.mult))
            link(V.tensor_scalar(baseT[:, :], baseT[:, :], -0.5, MAGIC, ALU.add, ALU.add))
            link(V.tensor_scalar(baseT[:, :], baseT[:, :], MAGIC, float(WBACK), ALU.subtract, ALU.subtract))
            dve.wait_ge(s_swin, 16 * UB)
            link(V.tensor_copy(swinf[:, :, :], swin[:, :, :]))
            for b in range(UB):
                link(V.tensor_scalar(junk[:, 0:SSTEP], swinf[:, b, :], thr_g[:, b:b + 1], None, ALU.is_lt, ALU.add, accum_out=pos[:, 1, b:b + 1]))
            link(V.tensor_tensor(pos[:, 2, :], pos[:, 0, :], pos[:, 1, :], ALU.add))
            link(V.tensor_scalar(pos[:, 2, :], pos[:, 2, :], float(E - WUSE), None, ALU.min))
            V.tensor_copy(idx_w[:, :], pos[:, 2, :]).then_inc(s_idxw, 1)
            dve.wait_ge(s_ev, 10)
            link(V.tensor_tensor(dlT[0:BLK, :], edgeT[0][0:BLK, :], baseT[0:BLK, :], ALU.subtract))
            link(V.memset(totals[:, :], 0.0))
            link(V.tensor_scalar(inT[0:BLK, :], dlT[0:BLK, :], 0.0, None, ALU.is_ge))
            V.scalar_tensor_tensor(baseT[0:BLK, :], dlT[0:BLK, :], float(WN), inT[0:BLK, :], ALU.is_lt, ALU.mult,
                                   accum_out=totals[0:BLK, 1:2]).then_inc(s_dl, 1)
            dve.wait_ge(s_const, 5)
            dve.wait_ge(s_bwin, 32 * UB)
            link(V.tensor_copy(swf[:, :, :], ewin[:, :, :]))
            link(V.tensor_copy(dwf[:, :, :], dwin[:, :, :]))
            link(V.tensor_scalar(hif[:, :, :], swf[:, :, :], 0.5, 1.0 / BLK, ALU.add, ALU.mult))
            link(V.tensor_scalar(hif[:, :, :], hif[:, :, :], -0.5, MAGIC, ALU.add, ALU.add))
            link(V.tensor_scalar(hif[:, :, :], hif[:, :, :], MAGIC, None, ALU.subtract))
            V.scalar_tensor_tensor(swf[:, :, :], hif[:, :, :], float(-BLK), swf[:, :, :], ALU.mult, ALU.add).then_inc(s_win, 1)
            for b in range(UB):
                link(V.tensor_scalar(dwf[:, b, :], dwf[:, b, :], thr_g[:, b:b + 1], None, ALU.subtract))
            link(V.memset(dwf[:, :, WUSE:WIN], -1.0))
            V.scalar_tensor_tensor(hif[:, :, :], dwf[:, :, :], float(NBLK), hif[:, :, :], ALU.mult, ALU.add).then_inc(s_win, 1)
            for b in range(UB):
                for k in range(BW):
                    link(V.tensor_scalar(junk[:, 0:WIN], dwf[:, b, :], float(k), None, ALU.is_equal, ALU.add, accum_out=deg[:, b, k:k + 1]))
            link(V.memset(totals[:, 2:4], 0.0))
            V.tensor_reduce(totals[:, 0:1], deg[:, :, :], AX.XY, ALU.add).then_inc(s_tot, 1)
            dve.wait_ge(s_tot, 1)
            V.memset(flagf[:, :], 0.0).then_inc(s_deg, 1)
            dve.wait_ge(s_sq, 1)
            V.reciprocal(deg[:, :, :], deg[:, :, :]).then_inc(s_dinv, 1)
            dve.wait_ge(s_ev, NJ)
            dve.wait_ge(s_win, 2)
            V.tensor_copy(flagf[:, 0:1], totals[:, 0:1]).then_inc(s_tot, 1)
            BANK0 = [0, 1, 2, 7, 0, 1, 2]

            def onehots(k, slot, first):
                if not first:
                    dve.wait_ge(s_blk, k - (SLOTS - 1))
                for a in range(2):
                    w = (P, QW)[a]
                    codes = sT[a][:, ds(k * 8, 8)]
                    V.tensor_tensor(hot[slot][a][:, 0:w, :], iota_v[:, 0:w, :],
                                    codes[:, None, :].broadcast_to([P, w, 8]), ALU.is_equal).then_inc(s_hot, 1)
            def scaled(l, t):
                b0, nb = blocks_of(t)[0], len(blocks_of(t))
                dve.wait_ge(s_w, NUB * l + t + 1)
                if t >= 3:
                    dve.wait_ge(s_u, NUB * l + t - 2)
                bank = BANK0[t] if l == 0 else 5 + t % 3
                wk = work[0:BLK, t % 3, 0:nb * D].rearrange("p (s d) -> p s d", d=D)
                V.tensor_tensor(wk, ps[0:BLK, bank, 0:nb * D].rearrange("p (s d) -> p s d", d=D),
                                dinv_col[0:BLK, b0:b0 + nb, None].broadcast_to([BLK, nb, D]), ALU.mult).then_inc(s_uf, 1)

            def parts(l):
                for t in range(NUB + 2):
                    if t < NUB:
                        scaled(l, t)
                    if 1 <= t <= NUB:
                        q = t - 1
                        b0, nb = blocks_of(q)[0], len(blocks_of(q))
                        dve.wait_ge(s_hi, NUB * l + q + 1)
                        wk = work[0:BLK, q % 3, 0:nb * D].rearrange("p (s d) -> p s d", d=D)
                        V.tensor_tensor(wk, wk, u[0:BLK, b0:b0 + nb, 0, :], ALU.subtract).then_inc(s_r1, 1)
                    if t >= 2:
                        q = t - 2
                        b0, nb = blocks_of(q)[0], len(blocks_of(q))
                        dve.wait_ge(s_mid, NUB * l + q + 1)
                        wk = work[0:BLK, q % 3, 0:nb * D].rearrange("p (s d) -> p s d", d=D)
                        V.tensor_tensor(u[0:BLK, b0:b0 + nb, 2, :], wk, u[0:BLK, b0:b0 + nb, 1, :], ALU.subtract).then_inc(s_u, 1)
                dve.wait_ge(s_u, NUB * l + NUB)

            def post(l, c):
                w, at = CW[c], CH * c
                z, m = work[:, 0, 0:w], work[:, 1, 0:w]
                h = hT[:, at:at + w]
                b = convb[:, ds(l, 1)]
                dve.wait_ge(s_agg, NCH * l + c + 1)
                V.tensor_tensor(z, ps[:, agg_bank(l, c), 0:w], dinv_all[:, at:at + w], ALU.mult).then_inc(s_rd, 1)
                dve.wait_ge(s_rd, 2 * NCH * l + 2 * c + 1)
                V.tensor_scalar(m, z, b, 0.0, ALU.add, ALU.min).then_inc(s_rd, 1)
                dve.wait_ge(s_rd, 2 * NCH * l + 2 * c + 2)
                link(V.tensor_scalar(z, z, b, 0.0, ALU.add, ALU.max))
                link(V.tensor_tensor(h, h, z, ALU.add))
                dve.wait_ge(s_exp, NCH * l + c + 1)
                V.scalar_tensor_tensor(h, m, -1.0, h, ALU.add, ALU.add).then_inc(s_h, 1)
                dve.wait_ge(s_h, NCH * l + c + 1)

            for i in range(GPC // 2):
                for k in (2 * i, 2 * i + 1):
                    onehots(k, k % SLOTS, k < SLOTS)
                if i == 1:
                    dve.wait_ge(s_dinvl, 32)
                if 1 <= i <= NUB:
                    scaled(0, i - 1)
            dve.wait_ge(s_u, NUB)
            for c in range(1, NCH):
                for slot in range(SLOTS):
                    onehots(GPC * c + slot, slot, False)
                if c == 2:
                    dve.wait_ge(s_hs, 16)
                if c >= 2:
                    post(0, c - 2)
                with dve.Fori(1, (GPC if c < NCH - 1 else LASTG) // SLOTS) as i:
                    for slot in range(SLOTS):
                        onehots(i * SLOTS + (GPC * c + slot), slot, False)
            onehots(NGRP - 1, 0, False)
            for c in (NCH - 2, NCH - 1):
                post(0, c)
            parts(1)
            dve.wait_ge(s_hs, 32)
            for c in range(NCH):
                V.tensor_reduce(most[:, c:c + 1], adj_codes[:, COFF[c]:COFF[c] + NBLK * SW[c]], AX.X, ALU.max).then_inc(s_most, 1)
                post(1, c)
            L = LAYERS - 1
            parts(L)
            dve.wait_ge(s_hs, 16 * LAYERS)

            def relation(r):
                link(V.scalar_tensor_tensor(relw[0:BLK, :], tyE[0:BLK, :], float(r), wE[0:BLK, :], ALU.is_equal, ALU.mult))
                for b in range(NB):
                    s = compB[0:BLK, r * NB + b:r * NB + b + 1]
                    if r == 0:
                        link(V.tensor_scalar(coef[0:BLK, :, b], relw[0:BLK, :], s, None, ALU.mult))
                    else:
                        link(V.scalar_tensor_tensor(coef[0:BLK, :, b], relw[0:BLK, :], s, coef[0:BLK, :, b], ALU.mult, ALU.add))
            done = 0
            for c in range(NCH):
                if c == NCH - 1:
                    dve.wait_ge(s_back[4], 16)
                    link(V.tensor_tensor(xb[0:BLK], xb[0:BLK], linbB[0:BLK, None, :].broadcast_to([BLK, NBLK, D]), ALU.add))
                post(L, c)
                if c == 1:
                    dve.wait_ge(s_back[1], 64)
                for _ in range((0, 2, 2, 2, 1, 1, 0)[c]):
                    relation(done)
                    done += 1
            dve.wait_ge(s_most, NCH)
            link(V.tensor_reduce(most[:, 7:8], most[:, 0:NCH], AX.X, ALU.max))
            V.tensor_scalar(totals[:, 2:3], most[:, 7:8], float(CODE8), float(E) / P, ALU.is_lt, ALU.mult).then_inc(s_tot, 1)
            dve.wait_ge(s_totp, 1)
            link(V.tensor_scalar(flagf[0:1, 0:3], ps[0:1, 7, 0:3], float(E), None, ALU.is_equal))
            link(V.tensor_tensor(flagf[0:1, 0:1], flagf[0:1, 0:1], flagf[0:1, 1:2], ALU.mult))
            link(V.tensor_tensor(flagf[0:1, 0:1], flagf[0:1, 0:1], flagf[0:1, 2:3], ALU.mult))
            V.tensor_copy(flag[0:1, 0:1], flagf[0:1, 0:1]).then_inc(s_flag, 1)
            for t in range(NUB + 1):
                if t < NUB:
                    b0, nb = blocks_of(t)[0], len(blocks_of(t))
                    dve.wait_ge(s_lin, t + 1)
                    y = xb[0:BLK, b0:b0 + nb, :]
                    link(V.tensor_tensor(y, ps[0:BLK, 5 + t % 3, 0:nb * D].rearrange("p (s d) -> p s d", d=D), y, ALU.add))
                    for q in range(nb):
                        link(V.bn_stats(bnst[0:BLK, q, 0:6], xb[0:BLK, b0 + q, :]))
                    for q in range(nb):
                        ins = V.bn_aggr(mv[0:BLK, b0 + q, :], bnst[0:BLK, q, 0:6])
                        ins.then_inc(s_var, 1) if q == nb - 1 else link(ins)
                    dve.wait_ge(s_var, t + 1)
                if t > 0:
                    b0, nb = blocks_of(t - 1)[0], len(blocks_of(t - 1))
                    dve.wait_ge(s_std, t)
                    link(V.reciprocal(rstd[0:BLK, b0:b0 + nb], rstd[0:BLK, b0:b0 + nb]))
                    for q in range(b0, b0 + nb):
                        ins = V.tensor_scalar(xb[0:BLK, q, :], xb[0:BLK, q, :], mv[0:BLK, q, 0:1], rstd[0:BLK, q:q + 1], ALU.subtract, ALU.mult)
                        ins.then_inc(s_x1, 1) if q == b0 + nb - 1 else link(ins)
            dve.wait_ge(s_x1, NUB)
            dve.wait_ge(s_back[0], 64)

            before = chain[0]
            dve.wait_ge(s_flag, 1)
            covered = dve.value_load(flag[0:1, 0:1], min_val=0, max_val=1)
            with dve.If(covered == 1):
                def indices(c, g):
                    V.tensor_copy(idxg[0:BLK, GG * g:GG * (g + 1)], srcI[0:BLK, ds(c * TPB + GG * g, GG)]).then_inc(s_idx, 1)
                for g in range(3):
                    indices(0, g)
                dve.wait_ge(s_zero, 3)

                def moving(c, j, first):
                    if not first:
                        dve.wait_ge(s_mu, c * TPB + (j - MS + 1))
                    V.scalar_tensor_tensor(mov[0:BLK, j % MS, :, :], iota_w[0:BLK, None, :].broadcast_to([BLK, NB, WN]),
                                           dl[0:BLK, ds(c * TPB + j, 1)],
                                           coef[0:BLK, ds(c * TPB + j, 1), :].rearrange("p t b -> p (t b)")[:, :, None].broadcast_to([BLK, NB, WN]),
                                           ALU.is_equal, ALU.mult).then_inc(s_m, 1)

                def fold(c):
                    dve.wait_ge(s_mu, c * TPB + TPB)
                    link(V.tensor_tensor(acc[:, :], ps[:, 0, 0:NB * BLK], carry[:, :], ALU.add))
                    V.tensor_copy(carry[:, :], ps[:, 1, 0:NB * BLK]).then_inc(s_fold, 1)
                    dve.wait_ge(s_fold, c + 1)

                def stats(c):
                    dve.wait_ge(s_fin, c + 1)
                    yv = ystage[0:BLK, 1, :]
                    link(V.tensor_tensor(yv, ps[0:BLK, 3, 0:D], xb[0:BLK, ds(c, 1), :].rearrange("p s d -> p (s d)"), ALU.add))
                    link(V.bn_stats(fst[0:BLK, 0:6], yv))
                    V.memset(fst[0:BLK, 10:11], 0.0)
                    V.bn_aggr(fst[0:BLK, 6:8], fst[0:BLK, 0:6]).then_inc(s_fv, 1)

                def norm(c, first):
                    dve.wait_ge(s_fs, c + 1)
                    link(V.reciprocal(fst[0:BLK, 9:10], fst[0:BLK, 8:9]))
                    if not first:
                        dve.wait_ge(s_out, c * 16)
                    V.tensor_scalar(ystage[0:BLK, 0, :], ystage[0:BLK, 1, :], fst[0:BLK, 6:7], fst[0:BLK, 9:10], ALU.subtract, ALU.mult).then_inc(s_y, 1)
                    dve.wait_ge(s_y, c + 1)

                def chunk(c, head, second=False, tail=True):
                    for j in range(TPB):
                        moving(c, j, head and j < MS)
                        if j == 1 and not head:
                            fold(c - 1)
                        if j == 8 and not head:
                            dve.wait_ge(s_mu, c * TPB + 6)
                            V.tensor_tensor(aggf[:, :, :].rearrange("p b n -> p (b n)"), ps[:, 2, 0:NB * BLK], acc[:, :], ALU.add).then_inc(s_af, 1)
                        if j == 17 and not head:
                            stats(c - 1)
                        if j == 21 and not head:
                            norm(c - 1, second)
                        for g in range(3):
                            if tail and j == min(GG * g + 5, TPB - 1):
                                dve.wait_ge(s_g[g], 16 * GG * (c + 1))
                                indices(c + 1, g)
                chunk(0, True)
                chunk(1, False, second=True)
                rolled(2, NBLK - 1, 4, lambda c: chunk(c, False))
                chunk(NBLK - 1, False, tail=False)
                fold(NBLK - 1)
                V.tensor_copy(aggf[:, :, :].rearrange("p b n -> p (b n)"), acc[:, :]).then_inc(s_af, 1)
                stats(NBLK - 1)
                norm(NBLK - 1, False)
            with dve.Else():
                chain[0] = before
                general_dve(dve, link)

        @block.tensor
        def _(pe):
            T = nc.tensor
            pe.wait_ge(s_const, 5)
            pe.wait_ge(s_cmp, NSMP)
            for b in range(UB):
                for k in range(NSMP):
                    last = T.matmul(ps[:, 7, b:b + 1], cmp[0:BLK, k, P * b:P * (b + 1)], ones[0:BLK, 0:1], start=(k == 0), stop=(k == NSMP - 1))
            last.then_inc(s_cnt, 1)
            n = 0

            def job(parts):
                nonlocal n
                if n >= 7:
                    pe.wait_ge(s_ev, n - 6)
                for o0, o1, src_ap, rows in parts:
                    last = T.transpose(ps[0:src_ap.shape[1], n % 7, o0:o1], src_ap, ident[0:rows, 0:rows])
                last.then_inc(s_job, 1)
                n += 1
            pe.wait_ge(s_wl, 64)
            job([(D * l, D * (l + 1), wst[:, l, :], P) for l in range(LAYERS)])
            job([(D * l, D * (l + 1), lst[:, D * l:D * (l + 1)], P) for l in range(LAYERS + 1)])
            for a in range(4):
                if a < 3:
                    pe.wait_ge(s_rawf, 2 * a + 2)
                else:
                    pe.wait_ge(s_raw[3], 32)
                job([(P * b, P * (b + 1), rawf[a][:, b, :], P) for b in range(4)])
                job([(P * b, P * (b + 1), rawf[a][:, 4 + b, :], P) for b in range(2)]
                    + [(2 * P, 2 * P + TAILR, rawf[a][0:TAILR, 6, :], TAILR)])
            pe.wait_ge(s_x, 16)
            for c in range(NCH):
                job([(BLK * q, BLK * (q + 1), xst[0:BLK, 4 * c + q, :], BLK) for q in range(min(4, NBLK - 4 * c))])
            for a, v in enumerate((swf, hif)):
                pe.wait_ge(s_win, a + 1)
                for q in range(3):
                    job([(256 * bb + P * h, 256 * bb + P * (h + 1), v[:, 2 * q + bb, P * h:P * (h + 1)], P)
                         for bb in range(min(2, UB - 2 * q)) for h in range(2)])
            pe.wait_ge(s_ev, NJ)

            pe.wait_ge(s_tot, 2)

            BANK0 = [0, 1, 2, 7, 0, 1, 2]

            def products(l, j):
                bank = BANK0[j] if l == 0 else 5 + j % 3
                for q, s in enumerate(blocks_of(j)):
                    last = T.matmul(ps[0:BLK, bank, D * q:D * (q + 1)], hT[:, BLK * s:BLK * (s + 1)],
                                    wT[:, l, :], start=True, stop=True)
                last.then_inc(s_w, 1)

            def build(k, slot, first):
                pe.wait_ge(s_hot, k * 2 + 2)
                if not first:
                    pe.wait_ge(s_adj, k - (SLOTS - 1))
                for g in range(GRP):
                    for h in range(2):
                        last = T.matmul(ps[:, 3 + slot, QW * g:QW * (g + 1)], hot[slot][0][:, :, 2 * g + h],
                                        hot[slot][1][:, 0:QW, 2 * g + h], start=(h == 0), stop=(h == 1))
                last.then_inc(s_blk, 1)

            def rows(l, c, s, first=False, end=False):
                region = adj[0:BLK, COFF[c]:COFF[c] + NBLK * SW[c]].rearrange("p (s n) -> p s n", s=NBLK)
                for k in range(3):
                    last = T.matmul(ps[:, agg_bank(l, c), 0:CW[c]], u[0:BLK, s, k, :], region[:, s, 0:CW[c]],
                                    start=(first and k == 0), stop=(end and k == 2))
                return last

            def own_loops(l, c):
                lo, end = CH * c, CH * c + CW[c]
                while lo < end:
                    s = lo // BLK
                    hi = min(end, BLK * (s + 1))
                    for k in range(3):
                        T.matmul(ps[:, agg_bank(l, c), lo - CH * c:hi - CH * c], u[0:BLK, s, k, :], identb[0:BLK, lo - BLK * s:hi - BLK * s],
                                 start=False, stop=False)
                    lo = hi

            for j in range(4):
                products(0, j)
            for i in range(GPC // 2):
                for k in (2 * i, 2 * i + 1):
                    build(k, k % SLOTS, k < SLOTS)
                if 3 <= i < NUB - 1:
                    pe.wait_ge(s_uf, i - 2)
                    products(0, i + 1)
            for c in range(1, NCH):
                pairs = (GPC if c < NCH - 1 else LASTG) // 2
                per = -(-(NBLK - 1) // pairs)
                build(GPC * c, 0, False)
                build(GPC * c + 1, 1, False)
                if c == 1:
                    pe.wait_ge(s_u, NUB)
                pe.wait_ge(s_adj, GPC * c)
                if c - 1 >= 3:
                    pe.wait_ge(s_rd, 2 * (c - 1 - 3) + 1)
                for q in range(per):
                    rows(0, c - 1, q, first=(q == 0))
                for i in range(1, pairs):
                    for k in (GPC * c + 2 * i, GPC * c + 2 * i + 1):
                        build(k, k % SLOTS, False)
                    for q in range(per):
                        rows(0, c - 1, i * per + q)
                if c == NCH - 1:
                    build(NGRP - 1, 0, False)
                own_loops(0, c - 1)
                rows(0, c - 1, NBLK - 1, end=True).then_inc(s_agg, 1)
            pe.wait_ge(s_adj, NGRP)
            pe.wait_ge(s_rd, 2 * (NCH - 1 - 3) + 1)
            for s in range(NBLK - 1):
                rows(0, NCH - 1, s, first=(s == 0))
            own_loops(0, NCH - 1)
            rows(0, NCH - 1, NBLK - 1, end=True).then_inc(s_agg, 1)

            for l in range(1, LAYERS):
                for j in range(NUB):
                    pe.wait_ge(s_h, l * NCH + (cover(j) - NCH))
                    if j >= 3:
                        pe.wait_ge(s_uf, NUB * l + j - 2)
                    products(l, j)
                for c in range(NCH):
                    if c >= 5:
                        pe.wait_ge(s_rd, 2 * NCH * l + 2 * (c - 5) + 1)
                    for s in range(NBLK - 1):
                        if c == 0 and s % UBT == 0:
                            pe.wait_ge(s_u, NUB * l + s // UBT + 1)
                        rows(l, c, s, first=(s == 0))
                    if c == 0:
                        pe.wait_ge(s_u, NUB * l + NUB)
                    own_loops(l, c)
                    rows(l, c, NBLK - 1, end=True).then_inc(s_agg, 1)
            pe.wait_ge(s_tot, 3)
            pe.wait_ge(s_dl, 1)
            T.matmul(ps[0:1, 7, 0:3], onesf[:, 0:1], totals[:, 0:3], start=True, stop=True).then_inc(s_totp, 1)
            pe.wait_ge(s_flag, 1)
            for r in range(3):
                pe.wait_ge(s_back[r], (64, 64, 16)[r])
            for j in range(NUB):
                pe.wait_ge(s_h, NCH * (LAYERS - 1) + cover(j))
                if j >= 3:
                    pe.wait_ge(s_var, j - 2)
                for q, s in enumerate(blocks_of(j)):
                    for k in range(LAYERS + 1):
                        hk = h_old[k] if k < LAYERS else hT
                        last = T.matmul(ps[0:BLK, 5 + j % 3, D * q:D * (q + 1)], hk[:, BLK * s:BLK * (s + 1)], linT[:, k, :],
                                        start=(k == 0), stop=(k == LAYERS))
                last.then_inc(s_lin, 1)
            pe.wait_ge(s_flag, 1)
            covered = pe.value_load(flag[0:1, 0:1], min_val=0, max_val=1)
            with pe.If(covered == 1):
                pe.wait_ge(s_zero, 3)
                pe.wait_ge(s_x1, NUB)
                NPREV = sum(1 for j in range(TPB) if LO[j] < 0)

                def tile(c, j):
                    if j % GG == 0:
                        pe.wait_ge(s_g[j // GG], 16 * GG * (c + 1))
                    pe.wait_ge(s_m, c * TPB + (j + 1))
                    cuts = [(2, LO[j], min(0, LO[j] + WN)), (0, max(0, LO[j]), min(BLK, LO[j] + WN)), (1, max(BLK, LO[j]), LO[j] + WN)]
                    off = {0: 0, 1: -BLK, 2: BLK}
                    for bank, a, b in cuts:
                        if a >= b:
                            continue
                        o = ps[:, bank, 0:NB * BLK].rearrange("p (b n) -> p b n", b=NB)[:, :, a + off[bank]:b + off[bank]]
                        last = T.matmul(o, gat[0:BLK, j, :], mov[0:BLK, j % MS, :, a - LO[j]:b - LO[j]], start=False, stop=False, skip_group_check=True)
                    last.then_inc(s_mu, 1)

                def finish(c):
                    pe.wait_ge(s_af, c + 1)
                    for b in range(NB):
                        last = T.matmul(ps[0:BLK, 3, 0:D], aggf[:, b, :], basesS[:, b, :], start=(b == 0), stop=(b == NB - 1))
                    last.then_inc(s_fin, 1)

                def chunk(c, head):
                    if not head:
                        pe.wait_ge(s_fold, c)
                    for bank in (2, 0, 1):
                        T.matmul(ps[:, bank, 0:NB * BLK], zeros[:, 0:P], zeros[:, 0:NB * BLK], start=True, stop=False, skip_group_check=True)
                    for j in range(TPB):
                        tile(c, j)
                        if j == 12 and not head:
                            finish(c - 1)
                chunk(0, True)
                with pe.Fori(1, NBLK) as c:
                    chunk(c, False)
                finish(NBLK - 1)
            with pe.Else():
                general_pe(pe)


_INS = ['x', 'src', 'dst', 'edge_type_8', 'edge_weight', 'L0_gnn_conv_w', 'L0_gnn_conv_b', 'L0_gnn_lin_w',
        'L0_gnn_lin_b', 'L1_gnn_bases', 'L1_gnn_w_comp']
_OUTS = [((3125, 128), 'float32')]


def kernel(**inputs):
    import numpy as _np
    import concourse.bacc as _bacc
    from concourse import mybir as _mybir
    from concourse.bass_utils import run_bass_kernel_spmd as _run

    nc = _bacc.Bacc("TRN2", target_bir_lowering=False, num_devices=1)
    arrays, args = {}, []
    for name in _INS:
        a = _np.ascontiguousarray(inputs[name])
        arrays[f"in_{name}_dram"] = a
        args.append(nc.dram_tensor(f"in_{name}_dram", a.shape, _mybir.dt.from_np(a.dtype), kind="ExternalInput").ap())
    for i, (shape, dtype) in enumerate(_OUTS):
        dt = _mybir.dt.from_np(_np.dtype(dtype))
        args.append(nc.dram_tensor(f"out_{i}_dram", shape, dt, kind="ExternalOutput").ap())
    build_program(nc, *args)
    r = _run(nc, [arrays], core_ids=[0])
    got = tuple(r.results[0][f"out_{i}_dram"] for i in range(len(_OUTS)))
    return got[0]
```
